# Optimizing a Trainium2 kernel written in Bass

```python
import numpy as np
import jax
import jax.numpy as jnp

def _softmax(x, axis=-1):
    return jax.nn.softmax(x, axis=axis)

def _gelu(x):
    return jax.nn.gelu(x, approximate=True)

def _silu(x):
    return jax.nn.silu(x)

def _sigmoid(x):
    return jax.nn.sigmoid(x)

def _layernorm(x, axis=-1, eps=1e-05):
    m = jnp.mean(x, axis=axis, keepdims=True)
    v = jnp.var(x, axis=axis, keepdims=True)
    return (x - m) / jnp.sqrt(v + eps)

def _scatter_add(tgt, idx, src, axis=0):
    return tgt.at[idx].add(src)

def _segment_sum(src, seg, n):
    return jax.ops.segment_sum(src, seg, n)
kernel_name = 'mk_xattn_ffn_d1_seqx_r4_82735a'

def setup_inputs(seed: int=0):
    np.random.seed(seed)
    _w = jnp.asarray

    def _rec_inputs():
        import jax
        import jax.numpy as jnp
        _rk = jax.random.key(seed)
        x = 7.22e-05 + 1 * jax.random.normal(jax.random.fold_in(_rk, 1), (16, 256, 256), jnp.float32)
        _lenS = 256 - jax.random.randint(jax.random.fold_in(_rk, 7), (16,), 0, max(1, 256 // 4) + 1, jnp.int32)
        _lenS2 = 256 - jax.random.randint(jax.random.fold_in(_rk, 8), (16,), 0, max(1, 256 // 4) + 1, jnp.int32)
        _ctx_1024P = jax.random.normal(jax.random.fold_in(_rk, 11), (16, 16, 256), jnp.float32)
        _ctx_1024c = jax.random.dirichlet(jax.random.fold_in(_rk, 511), 0.3 * jnp.ones((16,), jnp.float32), (16, 256))
        _ctx_1024t = jnp.einsum('bsk,bkd->bsd', _ctx_1024c, _ctx_1024P)
        _ctx_1024t = _ctx_1024t * jax.lax.rsqrt(jnp.mean(jnp.square(_ctx_1024t)) + 1e-12) * 0.953939
        ctx_1024 = 4.13588e-05 + 0.999923 * (_ctx_1024t + 0.3 * jax.random.normal(jax.random.fold_in(_rk, 611), (16, 256, 256), jnp.float32))
        return (x, ctx_1024)
    x, ctx_1024 = _rec_inputs()

    def _L0_xattn_setup():
        import jax, jax.numpy as jnp
        import numpy as np
        B, SD, SE, D, H = (4, 512, 512, 256, 16)
        HD = D // H

        def _mha(xq, xk, xv, Wq, bq, Wk, bk, Wv, bv, Wo, bo, causal):
            q = jnp.einsum('bsd,hde->bhse', xq, Wq) + bq[None, :, None, :]
            k = jnp.einsum('bsd,hde->bhse', xk, Wk) + bk[None, :, None, :]
            v = jnp.einsum('bsd,hde->bhse', xv, Wv) + bv[None, :, None, :]
            scale = 1.0 / jnp.sqrt(jnp.asarray(HD, q.dtype))
            scores = jnp.einsum('bhqe,bhke->bhqk', q, k) * scale
            if causal:
                mask = jnp.tril(jnp.ones((q.shape[2], k.shape[2]), bool))
                scores = jnp.where(mask, scores, jnp.finfo(scores.dtype).min)
            w = jax.nn.softmax(scores, axis=-1)
            out = jnp.einsum('bhqk,bhke->bhqe', w, v)
            out = out.transpose(0, 2, 1, 3).reshape(out.shape[0], out.shape[2], D)
            return out @ Wo + bo
        key = jax.random.key(seed)
        ks = jax.random.split(key, 19)
        sd = 1.0 / np.sqrt(D)
        n = lambda k, shape, s: jax.random.normal(k, shape, jnp.float32) * s
        inp = {'x': n(ks[0], (B, SD, D), 1.0), 'encoder_k': n(ks[1], (B, SE, D), 1.0), 'encoder_v': n(ks[2], (B, SE, D), 1.0), 'Wq1': n(ks[3], (H, D, HD), sd), 'bq1': jnp.zeros((H, HD), jnp.float32), 'Wk1': n(ks[4], (H, D, HD), sd), 'bk1': jnp.zeros((H, HD), jnp.float32), 'Wv1': n(ks[5], (H, D, HD), sd), 'bv1': jnp.zeros((H, HD), jnp.float32), 'Wo1': n(ks[6], (D, D), sd), 'bo1': jnp.zeros((D,), jnp.float32), 'Wq2': n(ks[7], (H, D, HD), sd), 'bq2': jnp.zeros((H, HD), jnp.float32), 'Wk2': n(ks[8], (H, D, HD), sd), 'bk2': jnp.zeros((H, HD), jnp.float32), 'Wv2': n(ks[9], (H, D, HD), sd), 'bv2': jnp.zeros((H, HD), jnp.float32), 'Wo2': n(ks[10], (D, D), sd), 'bo2': jnp.zeros((D,), jnp.float32)}
        return inp
    _L0_xattn_all = _L0_xattn_setup()
    _L0_xattn_in = {k: v for k, v in _L0_xattn_all.items() if k in ('Wq1', 'bq1', 'Wk1', 'bk1', 'Wv1', 'bv1', 'Wo1', 'bo1', 'Wq2', 'bq2', 'Wk2', 'bk2', 'Wv2', 'bv2', 'Wo2', 'bo2')}
    del _L0_xattn_all

    def _L0_ffn_setup():
        import jax, jax.numpy as jnp
        import numpy as np
        D_MODEL = 256
        N_EXPERTS = 8
        TOP_K = 2
        key = jax.random.key(seed)
        ks = jax.random.split(key, 8)
        d, e = (D_MODEL, N_EXPERTS)
        s = 1.0 / np.sqrt(d)
        return {'x': jax.random.normal(ks[0], (4, 512, d), dtype=jnp.float32), 'W_gate': jax.random.uniform(ks[1], (d, e), jnp.float32, -s, s), 'b_gate': jax.random.uniform(ks[2], (e,), jnp.float32, -s, s), 'W1': jax.random.uniform(ks[3], (e, d, d), jnp.float32, -s, s), 'b1': jax.random.uniform(ks[4], (e, d), jnp.float32, -s, s), 'W2': jax.random.uniform(ks[5], (e, d, d), jnp.float32, -s, s), 'b2': jax.random.uniform(ks[6], (e, d), jnp.float32, -s, s)}
    _L0_ffn_all = _L0_ffn_setup()
    _L0_ffn_in = {k: v for k, v in _L0_ffn_all.items() if k in ('W_gate', 'b_gate', 'W1', 'b1', 'W2', 'b2')}
    del _L0_ffn_all
    return {'x': x, 'ctx_1024': ctx_1024, 'L0_xattn_Wq1': _L0_xattn_in['Wq1'], 'L0_xattn_bq1': _L0_xattn_in['bq1'], 'L0_xattn_Wk1': _L0_xattn_in['Wk1'], 'L0_xattn_bk1': _L0_xattn_in['bk1'], 'L0_xattn_Wv1': _L0_xattn_in['Wv1'], 'L0_xattn_bv1': _L0_xattn_in['bv1'], 'L0_xattn_Wo1': _L0_xattn_in['Wo1'], 'L0_xattn_bo1': _L0_xattn_in['bo1'], 'L0_xattn_Wq2': _L0_xattn_in['Wq2'], 'L0_xattn_bq2': _L0_xattn_in['bq2'], 'L0_xattn_Wk2': _L0_xattn_in['Wk2'], 'L0_xattn_bk2': _L0_xattn_in['bk2'], 'L0_xattn_Wv2': _L0_xattn_in['Wv2'], 'L0_xattn_bv2': _L0_xattn_in['bv2'], 'L0_xattn_Wo2': _L0_xattn_in['Wo2'], 'L0_xattn_bo2': _L0_xattn_in['bo2'], 'L0_ffn_W_gate': _L0_ffn_in['W_gate'], 'L0_ffn_b_gate': _L0_ffn_in['b_gate'], 'L0_ffn_W1': _L0_ffn_in['W1'], 'L0_ffn_b1': _L0_ffn_in['b1'], 'L0_ffn_W2': _L0_ffn_in['W2'], 'L0_ffn_b2': _L0_ffn_in['b2']}

def reference(x, ctx_1024, L0_xattn_Wq1, L0_xattn_bq1, L0_xattn_Wk1, L0_xattn_bk1, L0_xattn_Wv1, L0_xattn_bv1, L0_xattn_Wo1, L0_xattn_bo1, L0_xattn_Wq2, L0_xattn_bq2, L0_xattn_Wk2, L0_xattn_bk2, L0_xattn_Wv2, L0_xattn_bv2, L0_xattn_Wo2, L0_xattn_bo2, L0_ffn_W_gate, L0_ffn_b_gate, L0_ffn_W1, L0_ffn_b1, L0_ffn_W2, L0_ffn_b2):
    import jax
    import jax.numpy as jnp

    def _L0_xattn_ref(x, encoder_k, encoder_v, Wq1, bq1, Wk1, bk1, Wv1, bv1, Wo1, bo1, Wq2, bq2, Wk2, bk2, Wv2, bv2, Wo2, bo2):
        import jax, jax.numpy as jnp
        import numpy as np
        B, SD, SE, D, H = (4, 512, 512, 256, 16)
        HD = D // H

        def _mha(xq, xk, xv, Wq, bq, Wk, bk, Wv, bv, Wo, bo, causal):
            q = jnp.einsum('bsd,hde->bhse', xq, Wq) + bq[None, :, None, :]
            k = jnp.einsum('bsd,hde->bhse', xk, Wk) + bk[None, :, None, :]
            v = jnp.einsum('bsd,hde->bhse', xv, Wv) + bv[None, :, None, :]
            scale = 1.0 / jnp.sqrt(jnp.asarray(HD, q.dtype))
            scores = jnp.einsum('bhqe,bhke->bhqk', q, k) * scale
            if causal:
                mask = jnp.tril(jnp.ones((q.shape[2], k.shape[2]), bool))
                scores = jnp.where(mask, scores, jnp.finfo(scores.dtype).min)
            w = jax.nn.softmax(scores, axis=-1)
            out = jnp.einsum('bhqk,bhke->bhqe', w, v)
            out = out.transpose(0, 2, 1, 3).reshape(out.shape[0], out.shape[2], D)
            return out @ Wo + bo
        h = _mha(x, x, x, Wq1, bq1, Wk1, bk1, Wv1, bv1, Wo1, bo1, causal=True)
        out = _mha(h, encoder_k, encoder_v, Wq2, bq2, Wk2, bk2, Wv2, bv2, Wo2, bo2, causal=False)
        return out

    def _L0_ffn_ref(x, W_gate, b_gate, W1, b1, W2, b2):
        import jax, jax.numpy as jnp
        import numpy as np
        D_MODEL = 256
        N_EXPERTS = 8
        TOP_K = 2
        B, T, d = x.shape
        xf = x.reshape(-1, d)
        scores = xf @ W_gate + b_gate
        topk_val, topk_idx = jax.lax.top_k(scores, TOP_K)
        onehot = jax.nn.one_hot(topk_idx, N_EXPERTS, dtype=xf.dtype)
        w = jnp.einsum('nk,nke->ne', topk_val, onehot)
        h = jax.nn.relu(jnp.einsum('nd,edh->neh', xf, W1) + b1)
        y = jnp.einsum('neh,ehd->ned', h, W2) + b2
        out = jnp.einsum('ned,ne->nd', y, w)
        return out.reshape(B, T, d)
    x = x + _L0_xattn_ref(_layernorm(x, axis=-1), ctx_1024, ctx_1024, L0_xattn_Wq1, L0_xattn_bq1, L0_xattn_Wk1, L0_xattn_bk1, L0_xattn_Wv1, L0_xattn_bv1, L0_xattn_Wo1, L0_xattn_bo1, L0_xattn_Wq2, L0_xattn_bq2, L0_xattn_Wk2, L0_xattn_bk2, L0_xattn_Wv2, L0_xattn_bv2, L0_xattn_Wo2, L0_xattn_bo2)
    x = x + _L0_ffn_ref(_layernorm(x, axis=-1), L0_ffn_W_gate, L0_ffn_b_gate, L0_ffn_W1, L0_ffn_b1, L0_ffn_W2, L0_ffn_b2)
    return x

_drawn_inputs = setup_inputs


def setup_inputs(seed=0):
    import zlib

    import numpy as np

    out = dict(_drawn_inputs(seed))
    spreads = {'L0_xattn_bq1': (0.0, 0.8),
     'L0_xattn_bk1': (0.0, 0.8),
     'L0_xattn_bv1': (0.0, 0.313),
     'L0_xattn_bo1': (0.0, 0.356),
     'L0_xattn_bq2': (0.0, 0.302),
     'L0_xattn_bk2': (0.0, 0.8),
     'L0_xattn_bv2': (0.0, 0.1),
     'L0_xattn_bo2': (0.0, 0.1)}
    factors = {'L0_ffn_b1': 4.44}
    for name, (base, spread) in spreads.items():
        noise = np.random.default_rng([zlib.crc32(name.encode()), seed]).standard_normal(out[name].shape)
        drawn = base * np.exp(spread * noise) if base else spread * noise
        out[name] = jnp.asarray(drawn.astype(out[name].dtype))
    for name, factor in factors.items():
        out[name] = (out[name] * factor).astype(out[name].dtype)
    return out
```

```python
from contextlib import ExitStack

import concourse.bass as bass
from concourse import mybir

F32 = mybir.dt.float32
F32R = mybir.dt.float32r
BF16 = mybir.dt.bfloat16
U32 = mybir.dt.uint32
ALU = mybir.AluOpType
ACT = mybir.ActivationFunctionType
AX = mybir.AxisListType

P = 128
B = 16
S = 256
D = 256
H = 16
HD = D // H
E = 8
EPS = 1e-5
C2 = D // P
HALF = H // 2
HI, LO = 0, 1
STACK = 3 * HD
ROWS = STACK + 2
QLO, QHI, KHI, KLO = 0, 1, 2, 3
BLOCKS = [(QHI, KHI), (QLO, KHI), (QHI, KLO)]
DMA_INC = 16
FILL_DMAS = 2 * len(BLOCKS)
MROW_DMAS = 4
MOVE_DMAS = 8
SMALL = 8
WQ1, WK1, WV1, WQO, WK2, WV2, WO2 = range(7)
BQ1, BK1, BQ2, BK2, BO1, B1 = 0, 2, 4, 6, 8, 10
NBCOL = B1 + 2 * E
IDENT, CAUSAL, EXPERTS, POWER = 0, P, 3 * P, 3 * P + E
NCONST = POWER + 2

JOBS = [
    (0, 0, "v2", -1, 0), (0, 1, "mtA", 0, 1), (0, 2, "xt", 1, 0), (0, 4, "q1", 1, 0), (0, 5, "k1", 1, 0),
    (0, 6, "wo", -2, 0), (0, 8, "ht", -2, 0), (0, 9, "mtB", -1, 0), (0, 9, "gate", -2, 0),
    (0, 10, "w1", -2, 0), (0, 11, "w1", -2, 1), (0, 12, "w2", -2, 0), (0, 12, "wt", -2, 0),
    (0, 13, "w1", -2, 2), (0, 14, "w2", -2, 1), (0, 15, "bw", -2, 0),
    (1, 0, "w1", -2, 3), (1, 1, "mtB", -1, 1), (1, 1, "w2", -2, 2), (1, 3, "v1", 1, 0), (1, 4, "w1", -2, 4),
    (1, 5, "w2", -2, 3), (1, 6, "q2", 0, 0), (1, 7, "w1", -2, 5), (1, 8, "k2", 0, 0), (1, 9, "mtA", 1, 0),
    (1, 10, "w2", -2, 4), (1, 11, "w1", -2, 6), (1, 12, "w2", -2, 5), (1, 13, "w1", -2, 7), (1, 14, "w2", -2, 6),
    (1, 15, "w2", -2, 7),
]
PER_SEQUENCE = {"mtA": 2, "mtB": 2, "w1": E, "w2": E}
NAMES = sorted({job[2] for job in JOBS})


def per(name):
    return PER_SEQUENCE.get(name, 1)


def at(p, k):
    return p[0] + k, p[1] + k


def exists(p):
    return 0 <= p[1] < B


def unit_before(layer, p):
    near, far = (("B", at(p, -2)), ("A", at(p, -1))) if layer == "A" else (("A", at(p, 1)), ("B", at(p, -1)))
    return near if exists(near[1]) else far if exists(far[1]) else None


def job_before(n, j):
    for back in range(1, 4 * len(JOBS)):
        turn, place = divmod(n - 2 * back, len(JOBS))
        _, _, name, off, number = JOBS[place]
        p = at(j, turn + off)
        if exists(p):
            return name, p, number
        if j[1] + turn < -1:
            return None
    return None


def steps_of(slot, step, j):
    return [(n, name, at(j, off), number) for n, (s, t, name, off, number) in enumerate(JOBS)
            if (s, t) == (slot, step) and exists(at(j, off))]


def iterations(engine, body, after_first=None):
    body((-1, -1))
    if after_first:
        after_first()
    for j in range(3):
        body((j, j))
    with engine.Fori(3, B - 2) as j:
        body((j, 7))
    for j in range(B - 2, B + 2):
        body((j, j))


def build(nc, x, ctxT, watt, w1, w2, wg, bcol, brow, bg, b2, const, out):
    ctx = ExitStack()
    with ctx:
        def sb(name, shape, dt):
            return ctx.enter_context(nc.sbuf_tensor(name, shape, dt))

        def sem(name):
            return ctx.enter_context(nc.semaphore(name))

        w_att = sb("w_att", [P, 7, 2, C2, D], F32R)
        w_up = sb("w_up", [P, E, 2, C2, D], F32R)
        w_down = sb("w_down", [P, E, 2, C2, D], F32R)
        wg_raw = sb("wg_raw", [P, C2, E], F32)
        wg_sb = sb("wg_sb", [P, 2, C2, E], F32R)
        bias = sb("bias", [P, NBCOL], F32)
        rows = sb("rows", [P, 3, D], F32)
        bg_sb = sb("bg_sb", [P, E], F32)
        b2_sb = sb("b2_sb", [E, D], F32)
        cst = sb("cst", [P, NCONST], F32)
        stack = {c: sb(f"stack{c}", [P, HALF, 2, S], F32R) for c in "AB"}
        staging = sb("staging", [P, 4, C2, S], F32R)
        val = {c: sb(f"val{c}", [P, 2, H, 2 * HD], F32) for c in "AB"}
        act_t = sb("act_t", [P, 2, C2, S], F32R)
        h_t = sb("h_t", [P, 2, C2, S], F32R)
        o_t = sb("o_t", [P, 2, C2, S], F32R)
        ctx_raw = sb("ctx_raw", [P, C2, S], F32)
        prob = sb("prob", [P, HALF, 2 * S], F32)
        hid = sb("hid", [P, 2, 2, C2, S], F32R)
        relu = sb("relu", [P, C2, S], F32)
        heads = sb("heads", [P, 8, S], F32)
        x_in = sb("x_in", [P, 2, D], F32)
        x_res = sb("x_res", [P, 2, D], F32)
        acc = sb("acc", [P, 2, D], F32)
        mx = {c: sb(f"mx{c}", [P, 2, H], F32) for c in "AB"}
        mrow = sb("mrow", [HALF, 2, S], F32R)
        stats = sb("stats", [P, 2, 6], F32)
        mv = sb("mv", [P, 2, 2], F32)
        rstd = sb("rstd", [P, 2], F32)
        gate = sb("gate", [P, 2, E], F32)
        top = sb("top", [P, 2, E], F32)
        top_at = sb("top_at", [P, 2, E], U32)
        top_f = sb("top_f", [P, 2, E], F32)
        first = sb("first", [P, 2, E], F32)
        second = sb("second", [P, 2, E], F32)
        wexp = sb("wexp", [P, 2, E], F32)
        wexp_t = sb("wexp_t", [E, S], F32)
        normed = prob

        def bank(name):
            return ctx.enter_context(nc.psum_tensor(name, [P, 512], F32))

        s_bank = [bank(f"s_bank{n}") for n in range(2)]
        t_bank = [bank(f"t_bank{n}") for n in range(2)]
        o_bank = [bank(f"o_bank{n}") for n in range(2)]
        g_bank = [bank(f"g_bank{n}") for n in range(2)]

        raw_in = [sem(f"raw_in{n}") for n in range(4)]
        small_in = sem("small_in")
        raw_hi = sem("raw_hi")
        raw_lo = sem("raw_lo")
        fold_done = sem("fold_done")
        folded_hi = sem("folded_hi")
        folded = sem("folded")
        ones_set = sem("ones_set")
        wg_split = sem("wg_split")
        x_loaded = sem("x_loaded")
        res_loaded = sem("res_loaded")
        ctx_loaded = sem("ctx_loaded")
        out_stored = sem("out_stored")
        ln1 = sem("ln1")
        ln2 = sem("ln2")
        ctx_split = sem("ctx_split")
        res_ready = sem("res_ready")
        acc_ready = sem("acc_ready")
        y_added = sem("y_added")
        gate_step = sem("gate_step")
        relu_done = sem("relu_done")
        hid_hi = sem("hid_hi")
        hid_lo = sem("hid_lo")
        filled = {(c, n): sem(f"filled{c}{n}") for c in "AB" for n in range(2)}
        s_done = {c: sem(f"s_done{c}") for c in "AB"}
        max_done = {c: sem(f"max_done{c}") for c in "AB"}
        mrow_in = {(c, n): sem(f"mrow_in{c}{n}") for c in "AB" for n in range(2)}
        st_done = {c: sem(f"st_done{c}") for c in "AB"}
        exp_done = {c: sem(f"exp_done{c}") for c in "AB"}
        masked = sem("masked")
        av_done = {c: sem(f"av_done{c}") for c in "AB"}
        heads_out = {c: sem(f"heads_out{c}") for c in "AB"}
        moved = {(c, n): sem(f"moved{c}{n}") for c in "AB" for n in range(2)}
        divided = {c: sem(f"divided{c}") for c in "AB"}
        o_hi = {c: sem(f"o_hi{c}") for c in "AB"}
        o_lo = {c: sem(f"o_lo{c}") for c in "AB"}
        done = {n: sem(f"{n}_done") for n in NAMES}
        high = {n: sem(f"{n}_high") for n in ("xt", "ht", "q1", "k1", "q2", "k2", "mtA", "mtB")}
        read = {n: sem(f"{n}_read") for n in NAMES}

        def count(name, p, number):
            return per(name) * p[0] + (number + 1)

        passed = sem("passed")

        def alone(engine):
            engine.sem_inc(passed, 1)

        block = ctx.enter_context(nc.Block())
        RAW = [("att", WQ1), ("att", WK1), ("att", WV1), ("att", WK2), ("att", WV2), ("att", WO2)]
        ATT = len(RAW)
        RAW += [(m, e) for e in range(E) for m in ("up", "down")]

        def raw_slot(n):
            return heads[:, 2 * (n % 4):2 * (n % 4) + 2, :]

        def split_to(kind, i, part):
            return {"att": w_att, "up": w_up, "down": w_down}[kind][:, i, part, :, :]

        @block.sync
        def _(sp):
            sp.dma_start(bias[:], bcol).then_inc(small_in, DMA_INC)
            sp.dma_start(cst[:], const).then_inc(small_in, DMA_INC)
            sp.dma_start(rows[:], brow.partition_broadcast(P)).then_inc(small_in, DMA_INC)
            sp.dma_start(bg_sb[:], bg.partition_broadcast(P)).then_inc(small_in, DMA_INC)
            sp.dma_start(b2_sb[:], b2).then_inc(small_in, DMA_INC)
            sp.dma_start(wg_raw[:], wg.rearrange("(c p) e -> p c e", p=P)).then_inc(small_in, DMA_INC)
            sp.dma_start(x_in[:], x[0].rearrange("(t p) d -> p t d", p=P)).then_inc(x_loaded, DMA_INC)
            sp.dma_start(relu[:], watt[7].rearrange("(c p) n -> p c n", p=P)).then_inc(small_in, DMA_INC)
            sp.dma_start(acc[:], watt[WQO].rearrange("(c p) n -> p c n", p=P)).then_inc(small_in, DMA_INC)
            def load_raw(n):
                kind, i = RAW[n]
                src = {"att": watt, "up": w1, "down": w2}[kind][i]
                if n >= 4:
                    sp.wait_ge(raw_lo, n - 3)
                sp.dma_start(raw_slot(n), src.rearrange("(c p) n -> p c n", p=P)).then_inc(raw_in[n % 4], DMA_INC)

            for n in range(ATT + 4):
                load_raw(n)
                if n == 1:
                    sp.dma_start(ctx_raw[:], ctxT[0].rearrange("(c p) s -> p c s", p=P)).then_inc(ctx_loaded, DMA_INC)

            def experts_weights():
                for n in range(ATT + 4, len(RAW)):
                    load_raw(n)
                sp.wait_ge(raw_lo, len(RAW))

            def fill(layer, p, half):
                for name in ("q1", "k1") if layer == "A" else ("q2", "k2"):
                    sp.wait_ge(read[name], p[0] + 1)
                if exists(at(p, -1)):
                    sp.wait_ge(st_done[layer], H * p[0] - HALF * (1 - half))
                for c in range(2):
                    for r, (q, k) in enumerate(BLOCKS):
                        low = (P // 2) * c + HD * r
                        sp.dma_start(
                            stack[layer][low:low + HD, 4 * half:4 * half + 4, :, :].bitcast(F32),
                            staging[(P // 2) * c:(P // 2) * (c + 1), q:k + 1:k - q, half, :].bitcast(F32),
                        ).then_inc(filled[layer, half], DMA_INC)

            def maxima(layer, p, half):
                sp.wait_ge(read["mt" + layer], 2 * p[0] + half + 1)
                for c in range(2):
                    for part in range(2):
                        row = (P // 2) * c + STACK + part
                        sp.dma_start(
                            stack[layer][row:row + 1, 4 * half:4 * half + 4, 0, :].bitcast(F32),
                            mrow[4 * c:4 * c + 4, part, :].bitcast(F32),
                        ).then_inc(mrow_in[layer, half], DMA_INC)

            def move(layer, p, half):
                sp.wait_ge(heads_out[layer], 2 * p[0] + half + 1)
                alone(sp)
                before = unit_before(layer, p)
                if before:
                    sp.wait_ge(o_lo[before[0]], 2 * before[1][0] + half + 1)
                for g in range(4):
                    for part in range(2):
                        sp.dma_start(
                            heads[32 * g:32 * g + 32, 4 + 2 * part + half, :],
                            heads[32 * g + HD * part:32 * g + HD * (part + 1), 2 * half:2 * half + 2, :],
                        ).then_inc(moved[layer, half], DMA_INC)

            def body(j):
                a, b, nxt, old = at(j, 0), at(j, -1), at(j, 1), at(j, -2)
                if exists(b):
                    fill("B", b, 1)
                if exists(old):
                    move("B", old, 1)
                if exists(a):
                    maxima("A", a, 1)
                if exists(at(j, 2)):
                    sp.wait_ge(done["xt"], j[0] + 2)
                    alone(sp)
                    sp.dma_start(x_in[:], x[j[0] + 2].rearrange("(t p) d -> p t d", p=P)).then_inc(x_loaded, DMA_INC)
                if exists(nxt):
                    fill("A", nxt, 0)
                if exists(b):
                    maxima("B", b, 0)
                if exists(a):
                    move("A", a, 0)
                if exists(b):
                    if exists(old):
                        sp.wait_ge(done["ht"], old[0] + 1)
                    alone(sp)
                    sp.dma_start(x_res[:], x[b[0]].rearrange("(t p) d -> p t d", p=P)).then_inc(res_loaded, DMA_INC)
                if exists(b):
                    maxima("B", b, 1)
                if exists(nxt):
                    fill("A", nxt, 1)
                if exists(a):
                    move("A", a, 1)
                if exists(nxt):
                    if exists(a):
                        sp.wait_ge(ctx_split, 2 * (a[0] + 1))
                        alone(sp)
                        sp.dma_start(ctx_raw[:], ctxT[nxt[0]].rearrange("(c p) s -> p c s", p=P)).then_inc(ctx_loaded, DMA_INC)
                if exists(a):
                    fill("B", a, 0)
                if exists(nxt):
                    maxima("A", nxt, 0)
                if exists(b):
                    move("B", b, 0)
                if exists(old):
                    sp.wait_ge(y_added, (E + 1) * (old[0] + 1))
                    alone(sp)
                    sp.dma_start(out[old[0]].rearrange("(t p) d -> p t d", p=P), acc[:]).then_inc(out_stored, DMA_INC)

            iterations(nc.sync, body, experts_weights)
            sp.wait_ge(out_stored, DMA_INC * B)

        @block.gpsimd
        def _(pool):
            for c in "AB":
                nc.gpsimd.memset(val[c][:], 1.0).then_inc(ones_set, 1)
                nc.gpsimd.memset(stack[c][:, :, :, :].bitcast(F32), -1.0).then_inc(ones_set, 1)
            pool.wait_ge(small_in, SMALL * DMA_INC)
            nc.gpsimd.tensor_copy(wg_sb[:, HI], wg_raw[:]).then_inc(wg_split, 1)
            pool.wait_ge(wg_split, 1)
            nc.gpsimd.tensor_tensor(wg_sb[:, LO], wg_raw[:], wg_sb[:, HI], ALU.subtract).then_inc(wg_split, 1)

            def split_context(p):
                pool.wait_ge(ctx_loaded, DMA_INC * (p[0] + 1))
                v1 = at(p, 1) if exists(at(p, 1)) else p
                pool.wait_ge(done["v1"], v1[0] + 1)
                if exists(at(p, -1)):
                    pool.wait_ge(done["v2"], p[0])
                alone(pool)
                nc.gpsimd.tensor_copy(act_t[:, HI], ctx_raw[:]).then_inc(ctx_split, 1)
                pool.wait_ge(ctx_split, 2 * p[0] + 1)
                nc.gpsimd.tensor_tensor(act_t[:, LO], ctx_raw[:], act_t[:, HI], ALU.subtract).then_inc(ctx_split, 1)

            def root(counter, p):
                pool.wait_ge(counter, 8 * p[0] + 5)
                nc.gpsimd.tensor_tensor(rstd[:], rstd[:], cst[:, POWER:POWER + 2], ALU.pow).then_inc(counter, 1)

            def attention_low(layer, p, half):
                pool.wait_ge(o_hi[layer], 2 * p[0] + half + 1)
                nc.gpsimd.tensor_tensor(o_t[:, LO, half], heads[:, 4 + half], o_t[:, HI, half], ALU.subtract) \
                    .then_inc(o_lo[layer], 1)

            def body(j):
                a, b, nxt, old = at(j, 0), at(j, -1), at(j, 1), at(j, -2)
                for slot in range(2):
                    for step in range(H):
                        if (slot, step) == (0, 0) and exists(nxt):
                            root(ln1, nxt)
                        if (slot, step) == (0, 6) and exists(old):
                            root(ln2, old)
                        if slot == 0 and exists(a):
                            pool.wait_ge(exp_done["A"], H * a[0] + step + 1)
                            diagonal = prob[:, step % HALF, P:3 * P].rearrange("p (b q) -> p b q", b=2)
                            alone(pool)
                            nc.gpsimd.affine_select(out=diagonal, in_=diagonal, compare_op=ALU.is_ge, fill=0.0, base=0,
                                                    pattern=[[0, 2], [1, P]], channel_multiplier=-1).then_inc(masked, 1)
                        for n, name, p, number in steps_of(slot, step, j):
                            if name == "w1":
                                pool.wait_ge(hid_hi, 2 * count("w1", p, number))
                                nc.gpsimd.tensor_tensor(hid[:, number % 2, LO], relu[:], hid[:, number % 2, HI],
                                                        ALU.subtract).then_inc(hid_lo, 1)
                        if (slot, step) == (0, 2) and exists(old):
                            attention_low("B", old, 1)
                        if (slot, step) == (0, 4) and exists(old):
                            pool.wait_ge(res_loaded, DMA_INC * (old[0] + 1))
                            for t in range(2):
                                nc.gpsimd.tensor_tensor(x_res[:, t], x_res[:, t], rows[:, 2], ALU.add).then_inc(res_ready, 1)
                        if (slot, step) == (0, 12) and exists(a):
                            attention_low("A", a, 0)
                        if (slot, step) == (1, 3) and exists(a):
                            attention_low("A", a, 1)
                            split_context(a)
                        if (slot, step) == (1, 12) and exists(b):
                            attention_low("B", b, 0)

            iterations(nc.gpsimd, body)

        def mrow_free(engine, name, p, number):
            c = name[-1]
            if number == 1:
                engine.wait_ge(mrow_in[c, 0], MROW_DMAS * DMA_INC * (p[0] + 1))
            else:
                before = unit_before(c, p)
                if before:
                    engine.wait_ge(mrow_in[before[0], 1], MROW_DMAS * DMA_INC * (before[1][0] + 1))

        def staging_free(engine, name, p):
            before = unit_before("A" if name[-1] == "1" else "B", p)
            if before:
                for half in range(2):
                    engine.wait_ge(filled[before[0], half], FILL_DMAS * DMA_INC * (before[1][0] + 1))

        @block.scalar
        def _(act):
            act.wait_ge(small_in, SMALL * DMA_INC)

            def raw_high(n):
                kind, i = RAW[n]
                act.wait_ge(raw_in[n % 4], DMA_INC * (n // 4 + 1))
                nc.scalar.activation(split_to(kind, i, HI), raw_slot(n), ACT.Copy).then_inc(raw_hi, 1)

            for n in range(ATT):
                raw_high(n)
            act.wait_ge(fold_done, 1)
            nc.scalar.activation(w_att[:, WQO, HI, :, :], g_bank[0][:, :].rearrange("p (c n) -> p c n", c=C2), ACT.Copy) \
                .then_inc(folded_hi, 1)

            def exponent(layer, p, h):
                act.wait_ge(st_done[layer], H * p[0] + h + 1)
                if h >= HALF:
                    act.wait_ge(av_done[layer], 4 * p[0] + h // 4 - 1)
                else:
                    before = unit_before(layer, p)
                    if before:
                        act.wait_ge(av_done[before[0]], 4 * before[1][0] + 3 + h // 4)
                low = P if layer == "A" else 0
                nc.scalar.activation(prob[:, h % HALF, low:], t_bank[h % 2][:, low:], ACT.Exp, scale=HD ** -0.5) \
                    .then_inc(exp_done[layer], 1)

            def heads_copy(layer, p, half):
                act.wait_ge(av_done[layer], 4 * p[0] + 2 * half + 2)
                before = unit_before(layer, p)
                if before:
                    act.wait_ge(moved[before[0], half], MOVE_DMAS * DMA_INC * (before[1][0] + 1))
                nc.scalar.activation(heads[:, 2 * half:2 * half + 2, :],
                                     o_bank[half][:, :].rearrange("p (g q) -> p g q", g=2), ACT.Copy) \
                    .then_inc(heads_out[layer], 1)

            def evacuate(n, name, p, number):
                g = g_bank[n % 2][:, :].rearrange("p (c s) -> p c s", c=2)
                if name not in high and name != "w1":
                    return
                act.wait_ge(done[name], count(name, p, number))
                if name in ("xt", "ht"):
                    if name == "xt" and exists(at(p, -2)):
                        act.wait_ge(done["v2"], p[0] - 1)
                    elif name == "xt" and exists(at(p, -1)):
                        act.wait_ge(done["v1"], p[0])
                    if name == "ht" and exists(at(p, -1)):
                        act.wait_ge(done["w1"], E * p[0])
                    nc.scalar.activation((act_t if name == "xt" else h_t)[:, HI], g, ACT.Copy).then_inc(high[name], 1)
                elif name in ("mtA", "mtB"):
                    mrow_free(act, name, p, number)
                    nc.scalar.activation(mrow[:, HI, :], g_bank[n % 2][0:HALF, 0:S], ACT.Copy).then_inc(high[name], 1)
                elif name == "w1":
                    if number or exists(at(p, -1)):
                        act.wait_ge(hid_lo, E * p[0] + number)
                    for c in range(C2):
                        nc.scalar.activation(relu[:, c, :], g[:, c, :], ACT.Relu,
                                             bias=bias[:, B1 + 2 * number + c:B1 + 2 * number + c + 1]).then_inc(relu_done, 1)
                    if number >= 2 or exists(at(p, -1)):
                        act.wait_ge(done["w2"], E * p[0] + number - 1)
                    for c in range(C2):
                        ins = nc.scalar.activation(hid[:, number % 2, HI, c, :], g[:, c, :], ACT.Relu,
                                                   bias=bias[:, B1 + 2 * number + c:B1 + 2 * number + c + 1])
                        ins.then_inc(hid_hi, 1)
                else:
                    col, place = {"q1": (BQ1, QHI), "k1": (BK1, KHI), "q2": (BQ2, QHI), "k2": (BK2, KHI)}[name]
                    staging_free(act, name, p)
                    for c in range(C2):
                        nc.scalar.activation(staging[:, place, c, :], g[:, c, :], ACT.Identity,
                                             bias=bias[:, col + c:col + c + 1]).then_inc(high[name], 1)

            def body(j):
                a, b, nxt, old = at(j, 0), at(j, -1), at(j, 1), at(j, -2)
                for slot in range(2):
                    layer, p = ("A", a) if slot == 0 else ("B", b)
                    for step in range(H):
                        if exists(p):
                            exponent(layer, p, step)
                        for job in steps_of(slot, step, j):
                            evacuate(*job)
                        if (slot, step) == (0, 1) and exists(old):
                            heads_copy("B", old, 1)
                        if (slot, step) == (0, 9) and exists(a):
                            heads_copy("A", a, 0)
                        if (slot, step) == (1, 1) and exists(a):
                            heads_copy("A", a, 1)
                        if (slot, step) == (1, 9) and exists(b):
                            heads_copy("B", b, 0)

            def experts_weights():
                for n in range(ATT, len(RAW)):
                    raw_high(n)

            iterations(nc.scalar, body, experts_weights)

        @block.vector
        def _(dve):
            dve.wait_ge(small_in, SMALL * DMA_INC)

            def raw_low(n):
                kind, i = RAW[n]
                dve.wait_ge(raw_hi, n + 1)
                nc.vector.tensor_tensor(split_to(kind, i, LO), raw_slot(n), split_to(kind, i, HI), ALU.subtract) \
                    .then_inc(raw_lo, 1)

            for n in range(ATT):
                raw_low(n)
            dve.wait_ge(folded_hi, 1)
            nc.vector.tensor_tensor(w_att[:, WQO, LO, :, :], g_bank[0][:, :].rearrange("p (c n) -> p c n", c=C2),
                                    w_att[:, WQO, HI, :, :], ALU.subtract).then_inc(folded, 1)
            dve.wait_ge(fold_done, 2)
            nc.vector.tensor_tensor(bias[:, BQ2:BQ2 + 2], g_bank[1][:, 0:2], bias[:, BQ2:BQ2 + 2], ALU.add).then_inc(folded, 1)

            def normalise(src, dst, counter, p):
                base = 8 * p[0]
                for t in range(2):
                    nc.vector.bn_stats(stats[:, t, :], src[:, t, :]).then_inc(counter, 1)
                dve.wait_ge(counter, base + 2)
                alone(dve)
                for t in range(2):
                    nc.vector.bn_aggr(mv[:, t, :], stats[:, t, :]).then_inc(counter, 1)
                dve.wait_ge(counter, base + 4)
                nc.vector.tensor_scalar(rstd[:, :], mv[:, :, 1], EPS, None, ALU.add).then_inc(counter, 1)
                dve.wait_ge(counter, base + 5)
                dve.wait_ge(counter, base + 6)
                for t in range(2):
                    nc.vector.tensor_scalar(dst[:, t, :], src[:, t, :], mv[:, t, 0:1], rstd[:, t:t + 1],
                                            ALU.subtract, ALU.mult).then_inc(counter, 1)

            def row_max(layer, p, h):
                dve.wait_ge(s_done[layer], H * p[0] + h + 1)
                if h % HALF == 0 and exists(at(p, -1)):
                    dve.wait_ge(done["mt" + layer], 2 * p[0] + h // HALF - 1)
                col = HALF * (h // HALF) + 4 * (h % 2) + h % HALF // 2
                s = s_bank[h % 2]
                if layer == "B":
                    nc.vector.tensor_reduce(mx["B"][:, :, col:col + 1], s[:, :].rearrange("p (c k) -> p c k", c=2),
                                            AX.X, ALU.max).then_inc(max_done["B"], 1)
                    return
                alone(dve)
                nc.vector.tensor_tensor_reduce(out=s[:, 0:P], in0=s[:, 0:P], in1=cst[:, CAUSAL + P:CAUSAL + 2 * P],
                                               scale=1.0, scalar=-3e38, op0=ALU.add, op1=ALU.max,
                                               accum_out=mx["A"][:, 0, col:col + 1])
                nc.vector.tensor_tensor_reduce(out=s[:, S:2 * S], in0=s[:, S:2 * S], in1=cst[:, CAUSAL:CAUSAL + 2 * P],
                                               scale=1.0, scalar=-3e38, op0=ALU.add, op1=ALU.max,
                                               accum_out=mx["A"][:, 1, col:col + 1]).then_inc(max_done["A"], 1)

            def divide(layer, p, half):
                dve.wait_ge(moved[layer, half], MOVE_DMAS * DMA_INC * (p[0] + 1))
                nc.vector.reciprocal(heads[:, 6 + half], heads[:, 6 + half]).then_inc(divided[layer], 1)
                dve.wait_ge(divided[layer], 4 * p[0] + 2 * half + 1)
                nc.vector.tensor_tensor(heads[:, 4 + half], heads[:, 4 + half], heads[:, 6 + half], ALU.mult) \
                    .then_inc(divided[layer], 1)
                dve.wait_ge(divided[layer], 4 * p[0] + 2 * half + 2)
                if layer == "A":
                    if exists(at(p, -2)):
                        dve.wait_ge(done["wo"], p[0] - 1)
                    elif exists(at(p, -1)):
                        dve.wait_ge(done["q2"], p[0])
                else:
                    reader = at(p, 1) if exists(at(p, 1)) else None
                    if reader:
                        dve.wait_ge(done["q2"], reader[0] + 1)
                    else:
                        dve.wait_ge(done["wo"], p[0])
                nc.vector.tensor_copy(o_t[:, HI, half], heads[:, 4 + half]).then_inc(o_hi[layer], 1)

            def evacuate(n, name, p, number):
                g = g_bank[n % 2][:, :].rearrange("p (c s) -> p c s", c=2)
                if name == "w1":
                    return
                dve.wait_ge(done[name], count(name, p, number))
                if name in ("xt", "ht"):
                    dve.wait_ge(high[name], p[0] + 1)
                    t = act_t if name == "xt" else h_t
                    nc.vector.tensor_tensor(t[:, LO], g, t[:, HI], ALU.subtract).then_inc(read[name], 1)
                elif name in ("mtA", "mtB"):
                    dve.wait_ge(high[name], count(name, p, number))
                    nc.vector.tensor_tensor(mrow[:, LO, :], g_bank[n % 2][0:HALF, 0:S], mrow[:, HI, :], ALU.subtract) \
                        .then_inc(read[name], 1)
                elif name in ("v1", "v2"):
                    layer = "A" if name == "v1" else "B"
                    if exists(at(p, -1)):
                        dve.wait_ge(av_done[layer], 4 * p[0])
                    for t in range(2):
                        ins = nc.vector.tensor_tensor(val[layer][:, t, :, 0:HD],
                                                      g[:, t, :].rearrange("p (h e) -> p h e", h=H),
                                                      rows[:, 0 if layer == "A" else 1, :].rearrange("p (h e) -> p h e", h=H),
                                                      ALU.add)
                    ins.then_inc(read[name], 1)
                elif name == "wo":
                    dve.wait_ge(res_ready, 2 * (p[0] + 1))
                    if exists(at(p, -1)):
                        dve.wait_ge(out_stored, DMA_INC * p[0])
                    nc.vector.tensor_tensor(acc[:], g, x_res[:], ALU.add).then_inc(read["wo"], 1)
                    dve.wait_ge(read["wo"], p[0] + 1)
                    normalise(acc, x_norm2, ln2, p)
                elif name == "gate":
                    gating(n, p)
                elif name == "wt":
                    if exists(at(p, -1)):
                        dve.wait_ge(done["bw"], p[0])
                    nc.vector.tensor_copy(wexp_t[:], g_bank[n % 2][0:E, 0:S]).then_inc(read["wt"], 1)
                elif name == "bw":
                    order = y_order.index(("bw", 0))
                    dve.wait_ge(y_added, (E + 1) * p[0] + order)
                    nc.vector.tensor_tensor(acc[:], g, acc[:], ALU.add).then_inc(y_added, 1)
                elif name == "w2":
                    order = y_order.index(("w2", number))
                    if order or exists(at(p, -1)):
                        dve.wait_ge(y_added, (E + 1) * p[0] + order)
                    for t in range(2):
                        ins = nc.vector.scalar_tensor_tensor(out=acc[:, t, :], in0=g[:, t, :],
                                                             scalar=wexp[:, t, number:number + 1], in1=acc[:, t, :],
                                                             op0=ALU.mult, op1=ALU.add)
                    ins.then_inc(y_added, 1)
                else:
                    col, hi, lo = {"q1": (BQ1, QHI, QLO), "k1": (BK1, KHI, KLO),
                                   "q2": (BQ2, QHI, QLO), "k2": (BK2, KHI, KLO)}[name]
                    dve.wait_ge(high[name], 2 * (p[0] + 1))
                    for c in range(C2):
                        ins = nc.vector.scalar_tensor_tensor(out=staging[:, lo, c, :], in0=g[:, c, :],
                                                             scalar=bias[:, col + c:col + c + 1], in1=staging[:, hi, c, :],
                                                             op0=ALU.add, op1=ALU.subtract)
                    ins.then_inc(read[name], 1)

            def gating(n, p):
                g = g_bank[n % 2][:, 0:2 * E].rearrange("p (t e) -> p t e", t=2)
                base = 9 * p[0]
                for t in range(2):
                    nc.vector.tensor_tensor(gate[:, t, :], g[:, t, :], bg_sb[:], ALU.add).then_inc(gate_step, 1)
                dve.wait_ge(gate_step, base + 2)
                alone(dve)
                for t in range(2):
                    nc.vector.max(top[:, t, :], gate[:, t, :]).then_inc(gate_step, 1)
                dve.wait_ge(gate_step, base + 4)
                alone(dve)
                for t in range(2):
                    nc.vector.max_index(top_at[:, t, :], top[:, t, :], gate[:, t, :]).then_inc(gate_step, 1)
                dve.wait_ge(gate_step, base + 6)
                nc.vector.tensor_copy(top_f[:], top_at[:]).then_inc(gate_step, 1)
                dve.wait_ge(gate_step, base + 7)
                for t in range(2):
                    for k, place in enumerate((first, second)):
                        ins = nc.vector.tensor_scalar(place[:, t, :], cst[:, EXPERTS:EXPERTS + E], top_f[:, t, k:k + 1],
                                                      top[:, t, k:k + 1], ALU.is_equal, ALU.mult)
                ins.then_inc(gate_step, 1)
                dve.wait_ge(gate_step, base + 8)
                nc.vector.tensor_tensor(wexp[:], first[:], second[:], ALU.add).then_inc(gate_step, 1)
                dve.wait_ge(gate_step, base + 9)

            y_order = [(name, number) for _, _, name, _, number in JOBS if name in ("w2", "bw")]
            x_norm2 = x_res

            def body(j):
                a, b, nxt, old = at(j, 0), at(j, -1), at(j, 1), at(j, -2)
                for slot in range(2):
                    layer, p = ("B", b) if slot == 0 else ("A", nxt)
                    for step in range(H):
                        if (slot, step) == (0, 0) and exists(nxt):
                            dve.wait_ge(x_loaded, DMA_INC * (nxt[0] + 1))
                            normalise(x_in, x_in, ln1, nxt)
                        if exists(p):
                            row_max(layer, p, step)
                        for job in steps_of(slot, step, j):
                            evacuate(*job)
                        if (slot, step) == (0, 2) and exists(old):
                            divide("B", old, 1)
                        if (slot, step) == (0, 12) and exists(a):
                            divide("A", a, 0)
                        if (slot, step) == (1, 3) and exists(a):
                            divide("A", a, 1)
                        if (slot, step) == (1, 12) and exists(b):
                            divide("B", b, 0)

            def experts_weights():
                for n in range(ATT, len(RAW)):
                    raw_low(n)

            iterations(nc.vector, body, experts_weights)

        @block.tensor
        def _(pe):
            pe.wait_ge(small_in, SMALL * DMA_INC)
            for o in range(C2):
                for c in range(C2):
                    last = nc.tensor.matmul(g_bank[0][:, o * D:(o + 1) * D], relu[:, c, o * P:(o + 1) * P], acc[:, c, :],
                                            start=(c == 0), stop=(c == C2 - 1))
            last.then_inc(fold_done, 1)
            for o in range(C2):
                for c in range(C2):
                    last = nc.tensor.matmul(g_bank[1][:, o:o + 1], acc[:, c, o * P:(o + 1) * P],
                                            bias[:, BO1 + c:BO1 + c + 1], start=(c == 0), stop=(c == C2 - 1))
            last.then_inc(fold_done, 1)
            pe.wait_ge(folded, 2)
            pe.wait_ge(raw_lo, ATT)
            pe.wait_ge(wg_split, 2)
            pe.wait_ge(ones_set, 4)

            def product(g, weights, data, weights_stay, width=D):
                still, moving = (weights, data) if weights_stay else (data, weights)
                for o in range(2):
                    for c in range(C2):
                        for a, b in ((HI, HI), (HI, LO), (LO, HI)):
                            last = nc.tensor.matmul(g[:, o * width:(o + 1) * width], still[:, a, c, o * P:(o + 1) * P],
                                                    moving[:, b, c, :], start=(c == 0 and a == b),
                                                    stop=(c == C2 - 1 and a == LO))
                return last

            def transpose_chunks(g, data):
                for t in range(2):
                    for c in range(C2):
                        last = nc.tensor.transpose(g[:, c * S + t * P:c * S + (t + 1) * P],
                                                   data[:, t, c * P:(c + 1) * P], cst[:, IDENT:IDENT + P])
                return last

            def job(n, name, p, number, j):
                g = g_bank[n % 2]
                before = job_before(n, j)
                if before:
                    name0, p0, number0 = before
                    if name0 == "w1":
                        pe.wait_ge(hid_hi, 2 * count("w1", p0, number0))
                    elif name0 in ("w2", "bw"):
                        pe.wait_ge(y_added, (E + 1) * p0[0] + y_place[(name0, number0)])
                    elif name0 == "gate":
                        pe.wait_ge(gate_step, 9 * p0[0] + 2)
                    else:
                        pe.wait_ge(read[name0], count(name0, p0, number0))
                if name == "xt":
                    pe.wait_ge(ln1, 8 * (p[0] + 1))
                    last = transpose_chunks(g, x_in)
                elif name == "ht":
                    pe.wait_ge(ln2, 8 * (p[0] + 1))
                    last = transpose_chunks(g, x_res)
                elif name in ("q1", "k1"):
                    pe.wait_ge(read["xt"], p[0] + 1)
                    last = product(g, w_att[:, WQ1 if name == "q1" else WK1], act_t, True)
                elif name == "v1":
                    pe.wait_ge(read["xt"], p[0] + 1)
                    last = product(g, w_att[:, WV1], act_t, False)
                elif name == "k2":
                    pe.wait_ge(ctx_split, 2 * (p[0] + 1))
                    last = product(g, w_att[:, WK2], act_t, True)
                elif name == "v2":
                    pe.wait_ge(ctx_split, 2 * (p[0] + 1))
                    last = product(g, w_att[:, WV2], act_t, False)
                elif name == "q2":
                    pe.wait_ge(o_lo["A"], 2 * (p[0] + 1))
                    last = product(g, w_att[:, WQO], o_t, True)
                elif name == "wo":
                    pe.wait_ge(o_lo["B"], 2 * (p[0] + 1))
                    last = product(g, w_att[:, WO2], o_t, False)
                elif name == "gate":
                    pe.wait_ge(read["ht"], p[0] + 1)
                    last = product(g, wg_sb, h_t, False, width=E)
                elif name == "w1":
                    pe.wait_ge(read["ht"], p[0] + 1)
                    if p[1] == 0:
                        pe.wait_ge(raw_lo, ATT + 2 * number + 1)
                    last = product(g, w_up[:, number], h_t, True)
                elif name == "w2":
                    pe.wait_ge(hid_lo, count("w2", p, number))
                    if p[1] == 0:
                        pe.wait_ge(raw_lo, ATT + 2 * number + 2)
                    last = product(g, w_down[:, number], hid[:, number % 2], False)
                elif name == "wt":
                    pe.wait_ge(gate_step, 9 * (p[0] + 1))
                    for t in range(2):
                        last = nc.tensor.transpose(g[0:E, t * P:(t + 1) * P], wexp[:, t, :], cst[:, IDENT:IDENT + P])
                elif name == "bw":
                    pe.wait_ge(read["wt"], p[0] + 1)
                    for t in range(2):
                        last = nc.tensor.matmul(g[:, t * D:(t + 1) * D], wexp_t[:, t * P:(t + 1) * P], b2_sb[:],
                                                start=True, stop=True)
                else:
                    layer = name[-1]
                    pe.wait_ge(max_done[layer], H * p[0] + HALF * (number + 1))
                    for t in range(2):
                        last = nc.tensor.transpose(g[0:HALF, t * P:(t + 1) * P],
                                                   mx[layer][:, t, HALF * number:HALF * (number + 1)],
                                                   cst[:, IDENT:IDENT + P])
                last.then_inc(done[name], 1)

            y_jobs = [(name, number) for _, _, name, _, number in JOBS if name in ("w2", "bw")]
            y_place = {y: n + 1 for n, y in enumerate(y_jobs)}

            def scores(layer, p, h):
                if h % HALF == 0:
                    pe.wait_ge(filled[layer, h // HALF], FILL_DMAS * DMA_INC * (p[0] + 1))
                if h >= 2:
                    pe.wait_ge(max_done[layer], H * p[0] + h - 1)
                else:
                    before = unit_before(layer, p)
                    if before:
                        pe.wait_ge(max_done[before[0]], H * before[1][0] + H - 1 + h)
                low, qk = (P // 2) * (h % 2), stack[layer]
                for c in range(2):
                    last = nc.tensor.matmul(s_bank[h % 2][:, c * S:(c + 1) * S],
                                            qk[low:low + STACK, h // 2, 0, c * P:(c + 1) * P],
                                            qk[low:low + STACK, h // 2, 1, :], start=True, stop=True)
                last.then_inc(s_done[layer], 1)

            def shifted(layer, p, h):
                if h % HALF == 0:
                    pe.wait_ge(mrow_in[layer, h // HALF], MROW_DMAS * DMA_INC * (p[0] + 1))
                if h >= 2:
                    pe.wait_ge(exp_done[layer], H * p[0] + h - 1)
                else:
                    before = unit_before(layer, p)
                    if before:
                        pe.wait_ge(exp_done[before[0]], H * before[1][0] + H - 1 + h)
                low, qk = (P // 2) * (h % 2), stack[layer]
                for c in range(2):
                    col = S * (1 - c if layer == "A" else c)
                    last = nc.tensor.matmul(t_bank[h % 2][:, col:col + S],
                                            qk[low:low + ROWS, h // 2, 1, c * P:(c + 1) * P],
                                            qk[low:low + ROWS, h // 2, 0, :], start=True, stop=True)
                last.then_inc(st_done[layer], 1)

            def values(layer, p, group):
                ready = masked if layer == "A" else exp_done["B"]
                pe.wait_ge(ready, H * p[0] + 4 * group + 4)
                if group == 0:
                    pe.wait_ge(read["v1" if layer == "A" else "v2"], p[0] + 1)
                if group % 2 == 0:
                    before = unit_before(layer, p)
                    if before:
                        pe.wait_ge(heads_out[before[0]], 2 * before[1][0] + group // 2 + 1)
                o = o_bank[group // 2]
                base = S * (group % 2)
                for c in range(2):
                    for i in range(4):
                        h = 4 * group + i
                        if layer == "A":
                            src = prob[:, h % HALF, S:2 * S] if c == 0 else prob[:, h % HALF, P:S]
                            lo = base + P * c
                        else:
                            src = prob[:, h % HALF, S * c:S * (c + 1)]
                            lo = base
                        last = nc.tensor.matmul(o[32 * i:32 * i + 32, lo:base + S], val[layer][:, c, h, :], src,
                                                start=(c == 0), stop=(c == 1), skip_group_check=True)
                last.then_inc(av_done[layer], 1)

            def body(j):
                a, b, nxt, old = at(j, 0), at(j, -1), at(j, 1), at(j, -2)
                for slot in range(2):
                    s_unit = ("B", b) if slot == 0 else ("A", nxt)
                    t_unit = ("A", a) if slot == 0 else ("B", b)
                    last_unit = ("B", old) if slot == 0 else ("A", a)
                    for step in range(H):
                        if exists(s_unit[1]):
                            scores(*s_unit, step)
                        if exists(t_unit[1]):
                            shifted(*t_unit, step)
                        for n, name, p, number in steps_of(slot, step, j):
                            job(n, name, p, number, j)
                        if step == 1 and exists(last_unit[1]):
                            values(*last_unit, 3)
                        if step in (5, 9, 13) and exists(t_unit[1]):
                            values(*t_unit, (step - 5) // 4)

            iterations(nc.tensor, body)


def kernel(x, ctx_1024, **w):
    import numpy as np
    import concourse.bacc as bacc
    from concourse import mybir as mb
    from concourse.bass_utils import run_bass_kernel_spmd

    def pick(name):
        return np.asarray(w["L0_" + name])

    halves, parity, elem, pair = np.meshgrid(range(2), range(2), range(HD), range(4), indexing="ij")
    order_qk = (HD * (8 * halves + 2 * pair + parity) + elem).reshape(-1)
    halves, place, elem, group = np.meshgrid(range(2), range(4), range(HD), range(2), indexing="ij")
    order_o = (HD * (4 * (2 * halves + group) + place) + elem).reshape(-1)

    def flat(name):
        return pick(name).transpose(1, 0, 2).reshape(D, D)

    watt = np.stack([
        flat("xattn_Wq1")[:, order_qk], flat("xattn_Wk1")[:, order_qk], flat("xattn_Wv1"),
        flat("xattn_Wq2")[:, order_qk], flat("xattn_Wk2")[:, order_qk], flat("xattn_Wv2"),
        pick("xattn_Wo2")[order_o, :], pick("xattn_Wo1")[order_o, :].T,
    ])

    def columns(v):
        return v.reshape(-1, P).T

    bcol = np.concatenate(
        [columns(pick("xattn_" + n).reshape(D)[order_qk]) for n in ("bq1", "bk1", "bq2", "bk2")]
        + [columns(pick("xattn_bo1")), columns(pick("ffn_b1"))], axis=1)
    brow = np.stack([pick("xattn_bv1").reshape(D), pick("xattn_bv2").reshape(D), pick("xattn_bo2")])
    before = np.arange(P)[:, None] >= np.arange(P)[None, :]
    const = np.concatenate([np.eye(P), np.zeros((P, P)), np.where(before, 0.0, -1e30),
                            np.tile(np.arange(E), (P, 1)), np.full((P, 2), -0.5)], axis=1).astype(np.float32)
    arrays = {
        "x": np.asarray(x), "ctxT": np.asarray(ctx_1024).transpose(0, 2, 1), "watt": watt,
        "w1": pick("ffn_W1"), "w2": pick("ffn_W2"), "wg": pick("ffn_W_gate"), "bcol": bcol, "brow": brow,
        "bg": pick("ffn_b_gate"), "b2": pick("ffn_b2"), "const": const,
    }
    arrays = {f"in_{k}": np.ascontiguousarray(v) for k, v in arrays.items()}
    nc = bacc.Bacc("TRN2", target_bir_lowering=False, num_devices=1)
    args = [nc.dram_tensor(k, v.shape, mb.dt.from_np(v.dtype), kind="ExternalInput").ap() for k, v in arrays.items()]
    out = nc.dram_tensor("out_y", (B, S, D), mb.dt.float32, kind="ExternalOutput").ap()
    build(nc, *args, out)
    r = run_bass_kernel_spmd(nc, [arrays], core_ids=[0])
    return r.results[0]["out_y"]
```

```python
from contextlib import ExitStack

import concourse.bass as bass
from concourse import mybir

F32 = mybir.dt.float32
F32R = mybir.dt.float32r
BF16 = mybir.dt.bfloat16
U32 = mybir.dt.uint32
ALU = mybir.AluOpType
ACT = mybir.ActivationFunctionType
AX = mybir.AxisListType

P = 128
B = 16
S = 256
D = 256
H = 16
HD = D // H
E = 8
EPS = 1e-5
C2 = D // P
HALF = H // 2
HI, LO = 0, 1
STACK = 3 * HD
ROWS = STACK + 1
QLO, QHI, KHI, KLO = 0, 1, 2, 3
BLOCKS = [(QHI, KHI), (QLO, KHI), (QHI, KLO)]
DMA_INC = 16
FILL_DMAS = 2 * len(BLOCKS)
SMALL = 8
WQ1, WK1, WV1, WQO, WK2, WV2, WO2 = range(7)
BQ1, BK1, BQ2, BK2, BO1, B1 = 0, 2, 4, 6, 8, 10
NBCOL = B1 + 2 * E
IDENT, CAUSAL, EXPERTS, POWER = 0, P, 3 * P, 3 * P + E
NCONST = POWER + 2

JOBS = [
    (0, 0, "v2", -1, 0), (0, 1, "mtA", 0, 1), (0, 2, "xt", 1, 0), (0, 3, "hdB", -2, 1), (0, 4, "q1", 1, 0),
    (0, 5, "otB", -2, 1), (0, 5, "k1", 1, 0), (0, 6, "wo", -2, 0), (0, 9, "mtB", -1, 0), (0, 9, "ht", -2, 0),
    (0, 10, "hdA", 0, 0), (0, 10, "gate", -2, 0), (0, 11, "w1", -2, 0), (0, 12, "otA", 0, 0), (0, 12, "w1", -2, 1),
    (0, 13, "w2", -2, 0), (0, 14, "w1", -2, 2), (0, 15, "w2", -2, 1),
    (1, 0, "w1", -2, 3), (1, 1, "mtB", -1, 1), (1, 1, "w2", -2, 2), (1, 2, "v1", 1, 0), (1, 3, "hdA", 0, 1),
    (1, 3, "w1", -2, 4), (1, 4, "w2", -2, 3), (1, 5, "otA", 0, 1), (1, 5, "w1", -2, 5), (1, 6, "q2", 0, 0),
    (1, 7, "w2", -2, 4), (1, 8, "k2", 0, 0), (1, 9, "mtA", 1, 0), (1, 9, "w1", -2, 6), (1, 10, "hdB", -1, 0),
    (1, 10, "w2", -2, 5), (1, 11, "w1", -2, 7), (1, 12, "otB", -1, 0), (1, 12, "w2", -2, 6), (1, 13, "wt", -2, 0),
    (1, 14, "bw", -2, 0), (1, 15, "w2", -2, 7),
]
PER_SEQUENCE = {"mtA": 2, "mtB": 2, "hdA": 2, "hdB": 2, "otA": 2, "otB": 2, "w1": E, "w2": E}
NAMES = sorted({job[2] for job in JOBS})


def per(name):
    return PER_SEQUENCE.get(name, 1)


def at(p, k):
    return p[0] + k, p[1] + k


def exists(p):
    return 0 <= p[1] < B


def unit_before(layer, p):
    near, far = (("B", at(p, -2)), ("A", at(p, -1))) if layer == "A" else (("A", at(p, 1)), ("B", at(p, -1)))
    return near if exists(near[1]) else far if exists(far[1]) else None


def job_before(n, j):
    for back in range(1, 4 * len(JOBS)):
        turn, place = divmod(n - 2 * back, len(JOBS))
        _, _, name, off, number = JOBS[place]
        p = at(j, turn + off)
        if exists(p):
            return name, p, number
        if j[1] + turn < -1:
            return None
    return None


def steps_of(slot, step, j):
    return [(n, name, at(j, off), number) for n, (s, t, name, off, number) in enumerate(JOBS)
            if (s, t) == (slot, step) and exists(at(j, off))]


def iterations(engine, body, after_first=None):
    body((-1, -1))
    if after_first:
        after_first()
    for j in range(3):
        body((j, j))
    with engine.Fori(3, B - 2) as j:
        body((j, 7))
    for j in range(B - 2, B + 2):
        body((j, j))


def build(nc, x, ctxT, watt, w1, w2, wg, bcol, brow, bg, b2, const, out):
    ctx = ExitStack()
    with ctx:
        def sb(name, shape, dt):
            return ctx.enter_context(nc.sbuf_tensor(name, shape, dt))

        def sem(name):
            return ctx.enter_context(nc.semaphore(name))

        w_att = sb("w_att", [P, 7, 2, C2, D], F32R)
        w_up = sb("w_up", [P, E, 2, C2, D], F32R)
        w_down = sb("w_down", [P, E, 2, C2, D], F32R)
        wg_raw = sb("wg_raw", [P, C2, E], F32)
        wg_sb = sb("wg_sb", [P, 2, C2, E], F32R)
        bias = sb("bias", [P, NBCOL], F32)
        rows = sb("rows", [P, 3, D], F32)
        bg_sb = sb("bg_sb", [P, E], F32)
        b2_sb = sb("b2_sb", [E, D], F32)
        cst = sb("cst", [P, NCONST], F32)
        stack = {c: sb(f"stack{c}", [P, HALF, 2, S], F32R) for c in "AB"}
        staging = sb("staging", [P, 4, C2, S], F32R)
        val = {c: sb(f"val{c}", [P, 2, H, 2 * HD], F32) for c in "AB"}
        act_t = sb("act_t", [P, 2, C2, S], F32R)
        h_t = sb("h_t", [P, 2, C2, S], F32R)
        o_t = sb("o_t", [P, 2, C2, S], F32R)
        ctx_raw = sb("ctx_raw", [P, C2, S], F32)
        prob = sb("prob", [P, HALF, 2 * S], F32)
        hid = sb("hid", [P, 2, 2, C2, S], F32R)
        relu = sb("relu", [P, 2, C2, S], F32)
        heads = sb("heads", [P, 8, S], F32)
        o_tok = heads[:, 4:6, :]
        x_in = sb("x_in", [P, 2, D], F32)
        x_res = sb("x_res", [P, 2, D], F32)
        acc = sb("acc", [P, 2, D], F32)
        mx = {c: sb(f"mx{c}", [P, 2, H], F32) for c in "AB"}
        mrow = sb("mrow", [HALF, S], F32R)
        rden = sb("rden", [P, H], F32)
        stats = sb("stats", [P, 2, 6], F32)
        mv = sb("mv", [P, 2, 2], F32)
        rstd = sb("rstd", [P, 2], F32)
        gate = sb("gate", [P, 2, E], F32)
        top = sb("top", [P, 2, E], F32)
        top_at = sb("top_at", [P, 2, E], U32)
        top_f = sb("top_f", [P, 2, E], F32)
        first = sb("first", [P, 2, E], F32)
        second = sb("second", [P, 2, E], F32)
        wexp = sb("wexp", [P, 2, E], F32)
        wexp_t = sb("wexp_t", [E, S], F32)
        normed = prob

        def bank(name):
            return ctx.enter_context(nc.psum_tensor(name, [P, 512], F32))

        s_bank = [bank(f"s_bank{n}") for n in range(2)]
        t_bank = [bank(f"t_bank{n}") for n in range(2)]
        o_bank = [bank(f"o_bank{n}") for n in range(2)]
        g_bank = [bank(f"g_bank{n}") for n in range(2)]

        raw_in = [sem(f"raw_in{n}") for n in range(4)]
        small_in = sem("small_in")
        raw_hi = sem("raw_hi")
        raw_lo = sem("raw_lo")
        fold_done = sem("fold_done")
        folded_hi = sem("folded_hi")
        folded = sem("folded")
        ones_set = sem("ones_set")
        wg_split = sem("wg_split")
        x_loaded = sem("x_loaded")
        res_loaded = sem("res_loaded")
        ctx_loaded = sem("ctx_loaded")
        out_stored = sem("out_stored")
        ln1 = sem("ln1")
        ln2 = sem("ln2")
        ctx_split = sem("ctx_split")
        res_ready = sem("res_ready")
        acc_ready = sem("acc_ready")
        y_added = sem("y_added")
        gate_step = sem("gate_step")
        relu_done = sem("relu_done")
        hid_hi = sem("hid_hi")
        hid_lo = sem("hid_lo")
        filled = {(c, n): sem(f"filled{c}{n}") for c in "AB" for n in range(2)}
        s_done = {c: sem(f"s_done{c}") for c in "AB"}
        max_done = {c: sem(f"max_done{c}") for c in "AB"}
        mrow_in = {(c, n): sem(f"mrow_in{c}{n}") for c in "AB" for n in range(2)}
        st_done = {c: sem(f"st_done{c}") for c in "AB"}
        exp_done = {c: sem(f"exp_done{c}") for c in "AB"}
        masked = sem("masked")
        av_done = {c: sem(f"av_done{c}") for c in "AB"}
        heads_out = {c: sem(f"heads_out{c}") for c in "AB"}
        inverted = {c: sem(f"inverted{c}") for c in "AB"}
        done = {n: sem(f"{n}_done") for n in NAMES}
        high = {n: sem(f"{n}_high") for n in ("xt", "ht", "q1", "k1", "q2", "k2", "otA", "otB")}
        read = {n: sem(f"{n}_read") for n in NAMES}

        def count(name, p, number):
            return per(name) * p[0] + (number + 1)

        passed = sem("passed")

        def alone(engine):
            engine.sem_inc(passed, 1)

        block = ctx.enter_context(nc.Block())
        RAW = [("att", WQ1), ("att", WK1), ("att", WV1), ("att", WK2), ("att", WV2), ("att", WO2)]
        ATT = len(RAW)
        RAW += [(m, e) for e in range(E) for m in ("up", "down")]

        def raw_slot(n):
            return heads[:, 2 * (n % 4):2 * (n % 4) + 2, :]

        def split_to(kind, i, part):
            return {"att": w_att, "up": w_up, "down": w_down}[kind][:, i, part, :, :]

        @block.sync
        def _(sp):
            sp.dma_start(bias[:], bcol).then_inc(small_in, DMA_INC)
            sp.dma_start(cst[:], const).then_inc(small_in, DMA_INC)
            sp.dma_start(rows[:], brow.partition_broadcast(P)).then_inc(small_in, DMA_INC)
            sp.dma_start(bg_sb[:], bg.partition_broadcast(P)).then_inc(small_in, DMA_INC)
            sp.dma_start(b2_sb[:], b2).then_inc(small_in, DMA_INC)
            sp.dma_start(wg_raw[:], wg.rearrange("(c p) e -> p c e", p=P)).then_inc(small_in, DMA_INC)
            sp.dma_start(x_in[:], x[0].rearrange("(t p) d -> p t d", p=P)).then_inc(x_loaded, DMA_INC)
            sp.dma_start(relu[:, 0], watt[7].rearrange("(c p) n -> p c n", p=P)).then_inc(small_in, DMA_INC)
            sp.dma_start(acc[:], watt[WQO].rearrange("(c p) n -> p c n", p=P)).then_inc(small_in, DMA_INC)
            def load_raw(n):
                kind, i = RAW[n]
                src = {"att": watt, "up": w1, "down": w2}[kind][i]
                if n >= 4:
                    sp.wait_ge(raw_lo, n - 3)
                sp.dma_start(raw_slot(n), src.rearrange("(c p) n -> p c n", p=P)).then_inc(raw_in[n % 4], DMA_INC)

            for n in range(ATT + 4):
                load_raw(n)
                if n == 1:
                    sp.dma_start(ctx_raw[:], ctxT[0].rearrange("(c p) s -> p c s", p=P)).then_inc(ctx_loaded, DMA_INC)

            def experts_weights():
                for n in range(ATT + 4, len(RAW)):
                    load_raw(n)
                sp.wait_ge(raw_lo, len(RAW))

            def fill(layer, p, half):
                for name in ("q1", "k1") if layer == "A" else ("q2", "k2"):
                    sp.wait_ge(read[name], p[0] + 1)
                if exists(at(p, -1)):
                    sp.wait_ge(st_done[layer], H * p[0] - HALF * (1 - half))
                for c in range(2):
                    for r, (q, k) in enumerate(BLOCKS):
                        low = (P // 2) * c + HD * r
                        sp.dma_start(
                            stack[layer][low:low + HD, 4 * half:4 * half + 4, :, :].bitcast(F32),
                            staging[(P // 2) * c:(P // 2) * (c + 1), q:k + 1:k - q, half, :].bitcast(F32),
                        ).then_inc(filled[layer, half], DMA_INC)

            def maxima(layer, p, half):
                sp.wait_ge(read["mt" + layer], 2 * p[0] + half + 1)
                sp.dma_start(stack[layer][STACK:STACK + P // 2 + 1:P // 2, 4 * half:4 * half + 4, 0, :].bitcast(F32),
                             mrow[:].bitcast(F32)).then_inc(mrow_in[layer, half], DMA_INC)

            def body(j):
                a, b, nxt, old = at(j, 0), at(j, -1), at(j, 1), at(j, -2)
                if exists(b):
                    fill("B", b, 1)
                if exists(a):
                    maxima("A", a, 1)
                if exists(at(j, 2)):
                    sp.wait_ge(done["xt"], j[0] + 2)
                    alone(sp)
                    sp.dma_start(x_in[:], x[j[0] + 2].rearrange("(t p) d -> p t d", p=P)).then_inc(x_loaded, DMA_INC)
                if exists(nxt):
                    fill("A", nxt, 0)
                if exists(b):
                    maxima("B", b, 0)
                if exists(b):
                    if exists(old):
                        sp.wait_ge(done["ht"], old[0] + 1)
                    alone(sp)
                    sp.dma_start(x_res[:], x[b[0]].rearrange("(t p) d -> p t d", p=P)).then_inc(res_loaded, DMA_INC)
                if exists(b):
                    maxima("B", b, 1)
                if exists(nxt):
                    fill("A", nxt, 1)
                if exists(nxt):
                    if exists(a):
                        sp.wait_ge(ctx_split, 2 * (a[0] + 1))
                        alone(sp)
                        sp.dma_start(ctx_raw[:], ctxT[nxt[0]].rearrange("(c p) s -> p c s", p=P)).then_inc(ctx_loaded, DMA_INC)
                if exists(a):
                    fill("B", a, 0)
                if exists(nxt):
                    maxima("A", nxt, 0)
                if exists(old):
                    sp.wait_ge(y_added, (E + 1) * (old[0] + 1))
                    alone(sp)
                    sp.dma_start(out[old[0]].rearrange("(t p) d -> p t d", p=P), acc[:]).then_inc(out_stored, DMA_INC)

            iterations(nc.sync, body, experts_weights)
            sp.wait_ge(out_stored, DMA_INC * B)

        @block.gpsimd
        def _(pool):
            for c in "AB":
                nc.gpsimd.memset(val[c][:], 1.0).then_inc(ones_set, 1)
                nc.gpsimd.memset(stack[c][:, :, :, :].bitcast(F32), -1.0).then_inc(ones_set, 1)
            pool.wait_ge(small_in, SMALL * DMA_INC)
            nc.gpsimd.tensor_copy(wg_sb[:, HI], wg_raw[:]).then_inc(wg_split, 1)
            pool.wait_ge(wg_split, 1)
            nc.gpsimd.tensor_tensor(wg_sb[:, LO], wg_raw[:], wg_sb[:, HI], ALU.subtract).then_inc(wg_split, 1)

            def split_context(p):
                pool.wait_ge(ctx_loaded, DMA_INC * (p[0] + 1))
                v1 = at(p, 1) if exists(at(p, 1)) else p
                pool.wait_ge(done["v1"], v1[0] + 1)
                if exists(at(p, -1)):
                    pool.wait_ge(done["v2"], p[0])
                alone(pool)
                nc.gpsimd.tensor_copy(act_t[:, HI], ctx_raw[:]).then_inc(ctx_split, 1)
                pool.wait_ge(ctx_split, 2 * p[0] + 1)
                nc.gpsimd.tensor_tensor(act_t[:, LO], ctx_raw[:], act_t[:, HI], ALU.subtract).then_inc(ctx_split, 1)

            def root(counter, p):
                pool.wait_ge(counter, 8 * p[0] + 5)
                nc.gpsimd.tensor_tensor(rstd[:], rstd[:], cst[:, POWER:POWER + 2], ALU.pow).then_inc(counter, 1)

            def body(j):
                a, b, nxt, old = at(j, 0), at(j, -1), at(j, 1), at(j, -2)
                for slot in range(2):
                    for step in range(H):
                        if (slot, step) == (0, 0) and exists(nxt):
                            root(ln1, nxt)
                        if (slot, step) == (0, 6) and exists(old):
                            root(ln2, old)
                        if slot == 0 and exists(a):
                            pool.wait_ge(exp_done["A"], H * a[0] + step + 1)
                            diagonal = prob[:, step % HALF, P:3 * P].rearrange("p (b q) -> p b q", b=2)
                            alone(pool)
                            nc.gpsimd.affine_select(out=diagonal, in_=diagonal, compare_op=ALU.is_ge, fill=0.0, base=0,
                                                    pattern=[[0, 2], [1, P]], channel_multiplier=-1).then_inc(masked, 1)
                        for n, name, p, number in steps_of(slot, step, j):
                            if name == "w1":
                                pool.wait_ge(hid_hi, 2 * count("w1", p, number))
                                nc.gpsimd.tensor_tensor(hid[:, number % 2, LO], relu[:, number % 2], hid[:, number % 2, HI],
                                                        ALU.subtract).then_inc(hid_lo, 1)
                        if (slot, step) == (0, 4) and exists(old):
                            pool.wait_ge(res_loaded, DMA_INC * (old[0] + 1))
                            for t in range(2):
                                nc.gpsimd.tensor_tensor(x_res[:, t], x_res[:, t], rows[:, 2], ALU.add).then_inc(res_ready, 1)
                        if (slot, step) == (1, 3) and exists(a):
                            split_context(a)

            iterations(nc.gpsimd, body)

        def mrow_free(engine, name, p, number):
            c = name[-1]
            if number == 1:
                engine.wait_ge(mrow_in[c, 0], DMA_INC * (p[0] + 1))
            else:
                before = unit_before(c, p)
                if before:
                    engine.wait_ge(mrow_in[before[0], 1], DMA_INC * (before[1][0] + 1))

        def o_t_free(engine, layer, p):
            if layer == "A":
                if exists(at(p, -2)):
                    engine.wait_ge(done["wo"], p[0] - 1)
                elif exists(at(p, -1)):
                    engine.wait_ge(done["q2"], p[0])
            elif exists(at(p, 1)):
                engine.wait_ge(done["q2"], p[0] + 2)
            else:
                engine.wait_ge(done["wo"], p[0])

        def staging_free(engine, name, p):
            before = unit_before("A" if name[-1] == "1" else "B", p)
            if before:
                for half in range(2):
                    engine.wait_ge(filled[before[0], half], FILL_DMAS * DMA_INC * (before[1][0] + 1))

        @block.scalar
        def _(act):
            act.wait_ge(small_in, SMALL * DMA_INC)

            def raw_high(n):
                kind, i = RAW[n]
                act.wait_ge(raw_in[n % 4], DMA_INC * (n // 4 + 1))
                nc.scalar.activation(split_to(kind, i, HI), raw_slot(n), ACT.Copy).then_inc(raw_hi, 1)

            for n in range(ATT):
                raw_high(n)
            act.wait_ge(fold_done, 1)
            nc.scalar.activation(w_att[:, WQO, HI, :, :], g_bank[0][:, :].rearrange("p (c n) -> p c n", c=C2), ACT.Copy) \
                .then_inc(folded_hi, 1)

            def exponent(layer, p, h):
                act.wait_ge(st_done[layer], H * p[0] + h + 1)
                if h >= HALF:
                    act.wait_ge(av_done[layer], 4 * p[0] + h // 4 - 1)
                else:
                    before = unit_before(layer, p)
                    if before:
                        act.wait_ge(av_done[before[0]], 4 * before[1][0] + 3 + h // 4)
                low = P if layer == "A" else 0
                nc.scalar.activation(prob[:, h % HALF, low:], t_bank[h % 2][:, low:], ACT.Exp, scale=HD ** -0.5) \
                    .then_inc(exp_done[layer], 1)

            def heads_copy(layer, p, half):
                act.wait_ge(av_done[layer], 4 * p[0] + 2 * half + 2)
                before = unit_before(layer, p)
                if before:
                    act.wait_ge(done["hd" + before[0]], 2 * before[1][0] + half + 1)
                nc.scalar.activation(heads[:, 2 * half:2 * half + 2, :],
                                     o_bank[half][:, :].rearrange("p (g q) -> p g q", g=2), ACT.Copy) \
                    .then_inc(heads_out[layer], 1)

            def evacuate(n, name, p, number):
                g = g_bank[n % 2][:, :].rearrange("p (c s) -> p c s", c=2)
                if name not in high and name not in ("w1", "mtA", "mtB"):
                    return
                act.wait_ge(done[name], count(name, p, number))
                if name in ("xt", "ht"):
                    if name == "xt" and exists(at(p, -2)):
                        act.wait_ge(done["v2"], p[0] - 1)
                    elif name == "xt" and exists(at(p, -1)):
                        act.wait_ge(done["v1"], p[0])
                    if name == "ht" and exists(at(p, -1)):
                        act.wait_ge(done["w1"], E * p[0])
                    nc.scalar.activation((act_t if name == "xt" else h_t)[:, HI], g, ACT.Copy).then_inc(high[name], 1)
                elif name in ("mtA", "mtB"):
                    mrow_free(act, name, p, number)
                    nc.scalar.activation(mrow[:], g_bank[n % 2][0:HALF, 0:S], ACT.Copy).then_inc(read[name], 1)
                elif name in ("otA", "otB"):
                    o_t_free(act, name[-1], p)
                    nc.scalar.activation(o_t[:, HI, number, :], g[:, 0, :], ACT.Copy).then_inc(high[name], 1)
                elif name == "w1":
                    if number >= 2 or exists(at(p, -1)):
                        act.wait_ge(hid_lo, E * p[0] + number - 1)
                    for c in range(C2):
                        nc.scalar.activation(relu[:, number % 2, c, :], g[:, c, :], ACT.Relu,
                                             bias=bias[:, B1 + 2 * number + c:B1 + 2 * number + c + 1]).then_inc(relu_done, 1)
                    if number >= 2 or exists(at(p, -1)):
                        act.wait_ge(done["w2"], E * p[0] + number - 1)
                    for c in range(C2):
                        ins = nc.scalar.activation(hid[:, number % 2, HI, c, :], g[:, c, :], ACT.Relu,
                                                   bias=bias[:, B1 + 2 * number + c:B1 + 2 * number + c + 1])
                        ins.then_inc(hid_hi, 1)
                else:
                    col, place = {"q1": (BQ1, QHI), "k1": (BK1, KHI), "q2": (BQ2, QHI), "k2": (BK2, KHI)}[name]
                    staging_free(act, name, p)
                    for c in range(C2):
                        nc.scalar.activation(staging[:, place, c, :], g[:, c, :], ACT.Identity,
                                             bias=bias[:, col + c:col + c + 1]).then_inc(high[name], 1)

            def body(j):
                a, b, nxt, old = at(j, 0), at(j, -1), at(j, 1), at(j, -2)
                for slot in range(2):
                    layer, p = ("A", a) if slot == 0 else ("B", b)
                    for step in range(H):
                        if exists(p):
                            exponent(layer, p, step)
                        for job in steps_of(slot, step, j):
                            evacuate(*job)
                        if (slot, step) == (0, 1) and exists(old):
                            heads_copy("B", old, 1)
                        if (slot, step) == (0, 9) and exists(a):
                            heads_copy("A", a, 0)
                        if (slot, step) == (1, 1) and exists(a):
                            heads_copy("A", a, 1)
                        if (slot, step) == (1, 9) and exists(b):
                            heads_copy("B", b, 0)

            def experts_weights():
                for n in range(ATT, len(RAW)):
                    raw_high(n)

            iterations(nc.scalar, body, experts_weights)

        @block.vector
        def _(dve):
            dve.wait_ge(small_in, SMALL * DMA_INC)

            def raw_low(n):
                kind, i = RAW[n]
                dve.wait_ge(raw_hi, n + 1)
                nc.vector.tensor_tensor(split_to(kind, i, LO), raw_slot(n), split_to(kind, i, HI), ALU.subtract) \
                    .then_inc(raw_lo, 1)

            for n in range(ATT):
                raw_low(n)
            dve.wait_ge(folded_hi, 1)
            nc.vector.tensor_tensor(w_att[:, WQO, LO, :, :], g_bank[0][:, :].rearrange("p (c n) -> p c n", c=C2),
                                    w_att[:, WQO, HI, :, :], ALU.subtract).then_inc(folded, 1)
            dve.wait_ge(fold_done, 2)
            nc.vector.tensor_tensor(bias[:, BQ2:BQ2 + 2], g_bank[1][:, 0:2], bias[:, BQ2:BQ2 + 2], ALU.add).then_inc(folded, 1)

            def normalise(src, dst, counter, p):
                base = 8 * p[0]
                for t in range(2):
                    nc.vector.bn_stats(stats[:, t, :], src[:, t, :]).then_inc(counter, 1)
                dve.wait_ge(counter, base + 2)
                alone(dve)
                for t in range(2):
                    nc.vector.bn_aggr(mv[:, t, :], stats[:, t, :]).then_inc(counter, 1)
                dve.wait_ge(counter, base + 4)
                nc.vector.tensor_scalar(rstd[:, :], mv[:, :, 1], EPS, None, ALU.add).then_inc(counter, 1)
                dve.wait_ge(counter, base + 5)
                dve.wait_ge(counter, base + 6)
                for t in range(2):
                    nc.vector.tensor_scalar(dst[:, t, :], src[:, t, :], mv[:, t, 0:1], rstd[:, t:t + 1],
                                            ALU.subtract, ALU.mult).then_inc(counter, 1)

            def row_max(layer, p, h):
                dve.wait_ge(s_done[layer], H * p[0] + h + 1)
                if h % HALF == 0 and exists(at(p, -1)):
                    dve.wait_ge(done["mt" + layer], 2 * p[0] + h // HALF - 1)
                col = HALF * (h // HALF) + 4 * (h % 2) + h % HALF // 2
                s = s_bank[h % 2]
                if layer == "B":
                    nc.vector.tensor_reduce(mx["B"][:, :, col:col + 1], s[:, :].rearrange("p (c k) -> p c k", c=2),
                                            AX.X, ALU.max).then_inc(max_done["B"], 1)
                    return
                alone(dve)
                nc.vector.tensor_tensor_reduce(out=s[:, 0:P], in0=s[:, 0:P], in1=cst[:, CAUSAL + P:CAUSAL + 2 * P],
                                               scale=1.0, scalar=-3e38, op0=ALU.add, op1=ALU.max,
                                               accum_out=mx["A"][:, 0, col:col + 1])
                nc.vector.tensor_tensor_reduce(out=s[:, S:2 * S], in0=s[:, S:2 * S], in1=cst[:, CAUSAL:CAUSAL + 2 * P],
                                               scale=1.0, scalar=-3e38, op0=ALU.add, op1=ALU.max,
                                               accum_out=mx["A"][:, 1, col:col + 1]).then_inc(max_done["A"], 1)

            def evacuate(n, name, p, number):
                g = g_bank[n % 2][:, :].rearrange("p (c s) -> p c s", c=2)
                if name in ("w1", "mtA", "mtB"):
                    return
                dve.wait_ge(done[name], count(name, p, number))
                if name in ("xt", "ht"):
                    dve.wait_ge(high[name], p[0] + 1)
                    t = act_t if name == "xt" else h_t
                    nc.vector.tensor_tensor(t[:, LO], g, t[:, HI], ALU.subtract).then_inc(read[name], 1)
                elif name in ("hdA", "hdB"):
                    layer = name[-1]
                    pairs = g_bank[n % 2][:, :].rearrange("p (h e) -> p h e", h=H)
                    nc.vector.reciprocal(rden[:, :].rearrange("p (h e) -> p h e", e=1), pairs[:, :, HD:HD + 1]) \
                        .then_inc(inverted[layer], 1)
                    before = unit_before(layer, p)
                    if before:
                        dve.wait_ge(done["ot" + before[0]], 2 * before[1][0] + number + 1)
                    dve.wait_ge(inverted[layer], count(name, p, number))
                    nc.vector.tensor_tensor(o_tok[:, number, :].rearrange("p (h e) -> p h e", h=H), pairs[:, :, 0:HD],
                                            rden[:, :].rearrange("p (h e) -> p h e", e=1).to_broadcast([P, H, HD]),
                                            ALU.mult).then_inc(read[name], 1)
                elif name in ("otA", "otB"):
                    dve.wait_ge(high[name], count(name, p, number))
                    nc.vector.tensor_tensor(o_t[:, LO, number, :], g[:, 0, :], o_t[:, HI, number, :], ALU.subtract) \
                        .then_inc(read[name], 1)
                elif name in ("v1", "v2"):
                    layer = "A" if name == "v1" else "B"
                    if exists(at(p, -1)):
                        dve.wait_ge(av_done[layer], 4 * p[0])
                    for t in range(2):
                        ins = nc.vector.tensor_tensor(val[layer][:, t, :, 0:HD],
                                                      g[:, t, :].rearrange("p (h e) -> p h e", h=H),
                                                      rows[:, 0 if layer == "A" else 1, :].rearrange("p (h e) -> p h e", h=H),
                                                      ALU.add)
                    ins.then_inc(read[name], 1)
                elif name == "wo":
                    dve.wait_ge(res_ready, 2 * (p[0] + 1))
                    if exists(at(p, -1)):
                        dve.wait_ge(out_stored, DMA_INC * p[0])
                    nc.vector.tensor_tensor(acc[:], g, x_res[:], ALU.add).then_inc(read["wo"], 1)
                    dve.wait_ge(read["wo"], p[0] + 1)
                    normalise(acc, x_norm2, ln2, p)
                elif name == "gate":
                    gating(n, p)
                elif name == "wt":
                    if exists(at(p, -1)):
                        dve.wait_ge(done["bw"], p[0])
                    nc.vector.tensor_copy(wexp_t[:], g_bank[n % 2][0:E, 0:S]).then_inc(read["wt"], 1)
                elif name == "bw":
                    order = y_order.index(("bw", 0))
                    dve.wait_ge(y_added, (E + 1) * p[0] + order)
                    nc.vector.tensor_tensor(acc[:], g, acc[:], ALU.add).then_inc(y_added, 1)
                elif name == "w2":
                    order = y_order.index(("w2", number))
                    if order or exists(at(p, -1)):
                        dve.wait_ge(y_added, (E + 1) * p[0] + order)
                    for t in range(2):
                        ins = nc.vector.scalar_tensor_tensor(out=acc[:, t, :], in0=g[:, t, :],
                                                             scalar=wexp[:, t, number:number + 1], in1=acc[:, t, :],
                                                             op0=ALU.mult, op1=ALU.add)
                    ins.then_inc(y_added, 1)
                else:
                    col, hi, lo = {"q1": (BQ1, QHI, QLO), "k1": (BK1, KHI, KLO),
                                   "q2": (BQ2, QHI, QLO), "k2": (BK2, KHI, KLO)}[name]
                    dve.wait_ge(high[name], 2 * (p[0] + 1))
                    for c in range(C2):
                        ins = nc.vector.scalar_tensor_tensor(out=staging[:, lo, c, :], in0=g[:, c, :],
                                                             scalar=bias[:, col + c:col + c + 1], in1=staging[:, hi, c, :],
                                                             op0=ALU.add, op1=ALU.subtract)
                    ins.then_inc(read[name], 1)

            def gating(n, p):
                g = g_bank[n % 2][:, 0:2 * E].rearrange("p (t e) -> p t e", t=2)
                base = 9 * p[0]
                for t in range(2):
                    nc.vector.tensor_tensor(gate[:, t, :], g[:, t, :], bg_sb[:], ALU.add).then_inc(gate_step, 1)
                dve.wait_ge(gate_step, base + 2)
                alone(dve)
                for t in range(2):
                    nc.vector.max(top[:, t, :], gate[:, t, :]).then_inc(gate_step, 1)
                dve.wait_ge(gate_step, base + 4)
                alone(dve)
                for t in range(2):
                    nc.vector.max_index(top_at[:, t, :], top[:, t, :], gate[:, t, :]).then_inc(gate_step, 1)
                dve.wait_ge(gate_step, base + 6)
                nc.vector.tensor_copy(top_f[:], top_at[:]).then_inc(gate_step, 1)
                dve.wait_ge(gate_step, base + 7)
                for t in range(2):
                    for k, place in enumerate((first, second)):
                        ins = nc.vector.tensor_scalar(place[:, t, :], cst[:, EXPERTS:EXPERTS + E], top_f[:, t, k:k + 1],
                                                      top[:, t, k:k + 1], ALU.is_equal, ALU.mult)
                ins.then_inc(gate_step, 1)
                dve.wait_ge(gate_step, base + 8)
                nc.vector.tensor_tensor(wexp[:], first[:], second[:], ALU.add).then_inc(gate_step, 1)
                dve.wait_ge(gate_step, base + 9)

            y_order = [(name, number) for _, _, name, _, number in JOBS if name in ("w2", "bw")]
            x_norm2 = x_res

            def body(j):
                a, b, nxt, old = at(j, 0), at(j, -1), at(j, 1), at(j, -2)
                for slot in range(2):
                    layer, p = ("B", b) if slot == 0 else ("A", nxt)
                    for step in range(H):
                        if (slot, step) == (0, 0) and exists(nxt):
                            dve.wait_ge(x_loaded, DMA_INC * (nxt[0] + 1))
                            normalise(x_in, x_in, ln1, nxt)
                        if exists(p):
                            row_max(layer, p, step)
                        for job in steps_of(slot, step, j):
                            evacuate(*job)

            def experts_weights():
                for n in range(ATT, len(RAW)):
                    raw_low(n)

            iterations(nc.vector, body, experts_weights)

        @block.tensor
        def _(pe):
            pe.wait_ge(small_in, SMALL * DMA_INC)
            for o in range(C2):
                for c in range(C2):
                    last = nc.tensor.matmul(g_bank[0][:, o * D:(o + 1) * D], relu[:, 0, c, o * P:(o + 1) * P], acc[:, c, :],
                                            start=(c == 0), stop=(c == C2 - 1))
            last.then_inc(fold_done, 1)
            for o in range(C2):
                for c in range(C2):
                    last = nc.tensor.matmul(g_bank[1][:, o:o + 1], acc[:, c, o * P:(o + 1) * P],
                                            bias[:, BO1 + c:BO1 + c + 1], start=(c == 0), stop=(c == C2 - 1))
            last.then_inc(fold_done, 1)
            pe.wait_ge(folded, 2)
            pe.wait_ge(raw_lo, ATT)
            pe.wait_ge(wg_split, 2)
            pe.wait_ge(ones_set, 4)

            def product(g, weights, data, weights_stay, width=D):
                still, moving = (weights, data) if weights_stay else (data, weights)
                for o in range(2):
                    for c in range(C2):
                        for a, b in ((HI, HI), (HI, LO), (LO, HI)):
                            last = nc.tensor.matmul(g[:, o * width:(o + 1) * width], still[:, a, c, o * P:(o + 1) * P],
                                                    moving[:, b, c, :], start=(c == 0 and a == b),
                                                    stop=(c == C2 - 1 and a == LO))
                return last

            def transpose_chunks(g, data):
                for t in range(2):
                    for c in range(C2):
                        last = nc.tensor.transpose(g[:, c * S + t * P:c * S + (t + 1) * P],
                                                   data[:, t, c * P:(c + 1) * P], cst[:, IDENT:IDENT + P])
                return last

            def job(n, name, p, number, j):
                g = g_bank[n % 2]
                before = job_before(n, j)
                if before:
                    name0, p0, number0 = before
                    if name0 == "w1":
                        pe.wait_ge(hid_hi, 2 * count("w1", p0, number0))
                    elif name0 in ("w2", "bw"):
                        pe.wait_ge(y_added, (E + 1) * p0[0] + y_place[(name0, number0)])
                    elif name0 == "gate":
                        pe.wait_ge(gate_step, 9 * p0[0] + 2)
                    else:
                        pe.wait_ge(read[name0], count(name0, p0, number0))
                if name == "xt":
                    pe.wait_ge(ln1, 8 * (p[0] + 1))
                    last = transpose_chunks(g, x_in)
                elif name == "ht":
                    pe.wait_ge(ln2, 8 * (p[0] + 1))
                    last = transpose_chunks(g, x_res)
                elif name in ("q1", "k1"):
                    pe.wait_ge(read["xt"], p[0] + 1)
                    last = product(g, w_att[:, WQ1 if name == "q1" else WK1], act_t, True)
                elif name == "v1":
                    pe.wait_ge(read["xt"], p[0] + 1)
                    last = product(g, w_att[:, WV1], act_t, False)
                elif name == "k2":
                    pe.wait_ge(ctx_split, 2 * (p[0] + 1))
                    last = product(g, w_att[:, WK2], act_t, True)
                elif name == "v2":
                    pe.wait_ge(ctx_split, 2 * (p[0] + 1))
                    last = product(g, w_att[:, WV2], act_t, False)
                elif name == "q2":
                    pe.wait_ge(read["otA"], 2 * (p[0] + 1))
                    last = product(g, w_att[:, WQO], o_t, True)
                elif name == "wo":
                    pe.wait_ge(read["otB"], 2 * (p[0] + 1))
                    last = product(g, w_att[:, WO2], o_t, False)
                elif name == "gate":
                    pe.wait_ge(read["ht"], p[0] + 1)
                    last = product(g, wg_sb, h_t, False, width=E)
                elif name == "w1":
                    pe.wait_ge(read["ht"], p[0] + 1)
                    if p[1] == 0:
                        pe.wait_ge(raw_lo, ATT + 2 * number + 1)
                    last = product(g, w_up[:, number], h_t, True)
                elif name == "w2":
                    pe.wait_ge(hid_lo, count("w2", p, number))
                    if p[1] == 0:
                        pe.wait_ge(raw_lo, ATT + 2 * number + 2)
                    last = product(g, w_down[:, number], hid[:, number % 2], False)
                elif name in ("hdA", "hdB"):
                    pe.wait_ge(heads_out[name[-1]], count(name, p, number))
                    for t in range(2):
                        for k in range(2):
                            last = nc.tensor.transpose(g[:, (2 * t + k) * P:(2 * t + k + 1) * P],
                                                       heads[:, 2 * number + k, t * P:(t + 1) * P],
                                                       cst[:, IDENT:IDENT + P])
                elif name in ("otA", "otB"):
                    pe.wait_ge(read["hd" + name[-1]], count(name, p, number))
                    for t in range(2):
                        last = nc.tensor.transpose(g[:, t * P:(t + 1) * P], o_tok[:, number, t * P:(t + 1) * P],
                                                   cst[:, IDENT:IDENT + P])
                elif name == "wt":
                    pe.wait_ge(gate_step, 9 * (p[0] + 1))
                    for t in range(2):
                        last = nc.tensor.transpose(g[0:E, t * P:(t + 1) * P], wexp[:, t, :], cst[:, IDENT:IDENT + P])
                elif name == "bw":
                    pe.wait_ge(read["wt"], p[0] + 1)
                    for t in range(2):
                        last = nc.tensor.matmul(g[:, t * D:(t + 1) * D], wexp_t[:, t * P:(t + 1) * P], b2_sb[:],
                                                start=True, stop=True)
                else:
                    layer = name[-1]
                    pe.wait_ge(max_done[layer], H * p[0] + HALF * (number + 1))
                    for t in range(2):
                        last = nc.tensor.transpose(g[0:HALF, t * P:(t + 1) * P],
                                                   mx[layer][:, t, HALF * number:HALF * (number + 1)],
                                                   cst[:, IDENT:IDENT + P])
                last.then_inc(done[name], 1)

            y_jobs = [(name, number) for _, _, name, _, number in JOBS if name in ("w2", "bw")]
            y_place = {y: n + 1 for n, y in enumerate(y_jobs)}

            def scores(layer, p, h):
                if h % HALF == 0:
                    pe.wait_ge(filled[layer, h // HALF], FILL_DMAS * DMA_INC * (p[0] + 1))
                if h >= 2:
                    pe.wait_ge(max_done[layer], H * p[0] + h - 1)
                else:
                    before = unit_before(layer, p)
                    if before:
                        pe.wait_ge(max_done[before[0]], H * before[1][0] + H - 1 + h)
                low, qk = (P // 2) * (h % 2), stack[layer]
                for c in range(2):
                    last = nc.tensor.matmul(s_bank[h % 2][:, c * S:(c + 1) * S],
                                            qk[low:low + STACK, h // 2, 0, c * P:(c + 1) * P],
                                            qk[low:low + STACK, h // 2, 1, :], start=True, stop=True)
                last.then_inc(s_done[layer], 1)

            def shifted(layer, p, h):
                if h % HALF == 0:
                    pe.wait_ge(mrow_in[layer, h // HALF], DMA_INC * (p[0] + 1))
                if h >= 2:
                    pe.wait_ge(exp_done[layer], H * p[0] + h - 1)
                else:
                    before = unit_before(layer, p)
                    if before:
                        pe.wait_ge(exp_done[before[0]], H * before[1][0] + H - 1 + h)
                low, qk = (P // 2) * (h % 2), stack[layer]
                for c in range(2):
                    col = S * (1 - c if layer == "A" else c)
                    last = nc.tensor.matmul(t_bank[h % 2][:, col:col + S],
                                            qk[low:low + ROWS, h // 2, 1, c * P:(c + 1) * P],
                                            qk[low:low + ROWS, h // 2, 0, :], start=True, stop=True)
                last.then_inc(st_done[layer], 1)

            def values(layer, p, group):
                ready = masked if layer == "A" else exp_done["B"]
                pe.wait_ge(ready, H * p[0] + 4 * group + 4)
                if group == 0:
                    pe.wait_ge(read["v1" if layer == "A" else "v2"], p[0] + 1)
                if group % 2 == 0:
                    before = unit_before(layer, p)
                    if before:
                        pe.wait_ge(heads_out[before[0]], 2 * before[1][0] + group // 2 + 1)
                o = o_bank[group // 2]
                base = S * (group % 2)
                for c in range(2):
                    for i in range(4):
                        h = 4 * group + i
                        if layer == "A":
                            src = prob[:, h % HALF, S:2 * S] if c == 0 else prob[:, h % HALF, P:S]
                            lo = base + P * c
                        else:
                            src = prob[:, h % HALF, S * c:S * (c + 1)]
                            lo = base
                        last = nc.tensor.matmul(o[32 * i:32 * i + 32, lo:base + S], val[layer][:, c, h, :], src,
                                                start=(c == 0), stop=(c == 1), skip_group_check=True)
                last.then_inc(av_done[layer], 1)

            def body(j):
                a, b, nxt, old = at(j, 0), at(j, -1), at(j, 1), at(j, -2)
                for slot in range(2):
                    s_unit = ("B", b) if slot == 0 else ("A", nxt)
                    t_unit = ("A", a) if slot == 0 else ("B", b)
                    last_unit = ("B", old) if slot == 0 else ("A", a)
                    for step in range(H):
                        if exists(s_unit[1]):
                            scores(*s_unit, step)
                        if exists(t_unit[1]):
                            shifted(*t_unit, step)
                        for n, name, p, number in steps_of(slot, step, j):
                            job(n, name, p, number, j)
                        if step == 1 and exists(last_unit[1]):
                            values(*last_unit, 3)
                        if step in (5, 9, 13) and exists(t_unit[1]):
                            values(*t_unit, (step - 5) // 4)

            iterations(nc.tensor, body)


def kernel(x, ctx_1024, **w):
    import numpy as np
    import concourse.bacc as bacc
    from concourse import mybir as mb
    from concourse.bass_utils import run_bass_kernel_spmd

    def pick(name):
        return np.asarray(w["L0_" + name])

    halves, parity, elem, pair = np.meshgrid(range(2), range(2), range(HD), range(4), indexing="ij")
    order_qk = (HD * (8 * halves + 2 * pair + parity) + elem).reshape(-1)
    def flat(name):
        return pick(name).transpose(1, 0, 2).reshape(D, D)

    watt = np.stack([
        flat("xattn_Wq1")[:, order_qk], flat("xattn_Wk1")[:, order_qk], flat("xattn_Wv1"),
        flat("xattn_Wq2")[:, order_qk], flat("xattn_Wk2")[:, order_qk], flat("xattn_Wv2"),
        pick("xattn_Wo2"), pick("xattn_Wo1").T,
    ])

    def columns(v):
        return v.reshape(-1, P).T

    bcol = np.concatenate(
        [columns(pick("xattn_" + n).reshape(D)[order_qk]) for n in ("bq1", "bk1", "bq2", "bk2")]
        + [columns(pick("xattn_bo1")), columns(pick("ffn_b1"))], axis=1)
    brow = np.stack([pick("xattn_bv1").reshape(D), pick("xattn_bv2").reshape(D), pick("xattn_bo2")])
    before = np.arange(P)[:, None] >= np.arange(P)[None, :]
    const = np.concatenate([np.eye(P), np.zeros((P, P)), np.where(before, 0.0, -1e30),
                            np.tile(np.arange(E), (P, 1)), np.full((P, 2), -0.5)], axis=1).astype(np.float32)
    arrays = {
        "x": np.asarray(x), "ctxT": np.asarray(ctx_1024).transpose(0, 2, 1), "watt": watt,
        "w1": pick("ffn_W1"), "w2": pick("ffn_W2"), "wg": pick("ffn_W_gate"), "bcol": bcol, "brow": brow,
        "bg": pick("ffn_b_gate"), "b2": pick("ffn_b2"), "const": const,
    }
    arrays = {f"in_{k}": np.ascontiguousarray(v) for k, v in arrays.items()}
    nc = bacc.Bacc("TRN2", target_bir_lowering=False, num_devices=1)
    args = [nc.dram_tensor(k, v.shape, mb.dt.from_np(v.dtype), kind="ExternalInput").ap() for k, v in arrays.items()]
    out = nc.dram_tensor("out_y", (B, S, D), mb.dt.float32, kind="ExternalOutput").ap()
    build(nc, *args, out)
    r = run_bass_kernel_spmd(nc, [arrays], core_ids=[0])
    return r.results[0]["out_y"]
```

```python
from contextlib import ExitStack

import concourse.bass as bass
from concourse import mybir

F32 = mybir.dt.float32
F32R = mybir.dt.float32r
U32 = mybir.dt.uint32
ALU = mybir.AluOpType
ACT = mybir.ActivationFunctionType
AX = mybir.AxisListType

P = 128
B = 16
S = 256
D = 256
H = 16
HD = D // H
E = 8
EPS = 1e-5
C2 = D // P
HALF = H // 2
HI, LO = 0, 1
STACK = 3 * HD
ROWS = STACK + 1
QLO, QHI, KHI, KLO = 0, 1, 2, 3
BLOCKS = [(QHI, KHI), (QLO, KHI), (QHI, KLO)]
DMA_INC = 16
FILL_DMAS = 2 * len(BLOCKS)
FIRST, SMALL = 2, 7
WQ1, WK1, WV1, WQO, WK2, WV2, WO2 = range(7)
BQ1, BK1, BQ2, BK2, BO1, B1, BG = 0, 2, 4, 6, 8, 10, 10 + 2 * E
NBCOL = BG + 1
GATE_STEPS = 10
IDENT, CAUSAL, EXPERTS, POWER = 0, P, 3 * P, 3 * P + E
NCONST = POWER + 2

JOBS = [
    (0, 0, 1, "w2", -3, 5), (0, 1, 2, "mtA", 0, 1), (0, 2, 0, "v2", -1, 0), (0, 3, 1, "hdB", -2, 1),
    (0, 3, 2, "w1", -3, 7), (0, 4, 0, "xt", 1, 0), (0, 4, 1, "w2", -3, 6), (0, 5, 2, "otB", -2, 1),
    (0, 6, 0, "q1", 1, 0), (0, 7, 1, "wo", -2, 0), (0, 8, 2, "k1", 1, 0), (0, 10, 0, "w2", -3, 7),
    (0, 10, 1, "ht", -2, 0), (0, 11, 2, "hdA", 0, 0), (0, 12, 0, "mtB", -1, 0), (0, 12, 1, "w1", -2, 0),
    (0, 13, 2, "gate", -2, 0), (0, 13, 0, "otA", 0, 0), (0, 14, 1, "gt", -2, 0), (0, 14, 2, "w1", -2, 1),
    (0, 15, 0, "w2", -2, 0),
    (1, 0, 1, "w1", -2, 2), (1, 1, 2, "wt", -2, 0), (1, 2, 0, "mtB", -1, 1), (1, 2, 1, "v1", 1, 0),
    (1, 3, 2, "hdA", 0, 1), (1, 3, 0, "w2", -2, 1), (1, 4, 1, "w1", -2, 3), (1, 5, 2, "otA", 0, 1),
    (1, 6, 0, "k2", 0, 0), (1, 7, 1, "w2", -2, 2), (1, 7, 2, "bw", -2, 0), (1, 8, 0, "q2", 0, 0),
    (1, 10, 1, "mtA", 1, 0), (1, 10, 0, "w1", -2, 4), (1, 11, 1, "hdB", -1, 0), (1, 11, 2, "w2", -2, 3),
    (1, 12, 0, "w1", -2, 5), (1, 13, 1, "otB", -1, 0), (1, 14, 2, "w2", -2, 4), (1, 15, 0, "w1", -2, 6),
]
PER_SEQUENCE = {"mtA": 2, "mtB": 2, "hdA": 2, "hdB": 2, "otA": 2, "otB": 2, "w1": E, "w2": E}
NAMES = sorted({job[3] for job in JOBS})


def per(name):
    return PER_SEQUENCE.get(name, 1)


def at(p, k):
    return p[0] + k, p[1] + k


def exists(p):
    return 0 <= p[1] < B


def unit_before(layer, p):
    near, far = (("B", at(p, -2)), ("A", at(p, -1))) if layer == "A" else (("A", at(p, 1)), ("B", at(p, -1)))
    return near if exists(near[1]) else far if exists(far[1]) else None


def job_before(n, j):
    for back in range(1, 4 * len(JOBS)):
        turn, place = divmod(n - back, len(JOBS))
        _, _, bank, name, off, number = JOBS[place]
        p = at(j, turn + off)
        if bank == JOBS[n][2] and exists(p):
            return name, p, number
        if j[1] + turn < -1:
            return None
    return None


def steps_of(slot, step, j):
    return [(n, name, at(j, off), number) for n, (s, t, _, name, off, number) in enumerate(JOBS)
            if (s, t) == (slot, step) and exists(at(j, off))]


def jobs_before(slot, step, j):
    if step or slot:
        return steps_of(*((slot, step - 1) if step else (0, H - 1)), j)
    return steps_of(1, H - 1, at(j, -1))


def iterations(engine, body):
    for j in range(-1, 4):
        body((j, j))
    with engine.Fori(4, B - 2) as j:
        body((j, 8))
    for j in range(B - 2, B + 3):
        body((j, j))


def build(nc, x, ctxT, watt, w1, w2, wg, bcol, brow, b2, const, out):
    ctx = ExitStack()
    with ctx:
        def sb(name, shape, dt):
            return ctx.enter_context(nc.sbuf_tensor(name, shape, dt))

        def sem(name):
            return ctx.enter_context(nc.semaphore(name))

        w_att = sb("w_att", [P, 7, 2, C2, D], F32R)
        w_up = sb("w_up", [P, E, 2, C2, D], F32R)
        w_down = sb("w_down", [P, E, 2, C2, D], F32R)
        wg_raw = sb("wg_raw", [P, C2, E], F32)
        wg_flat = sb("wg_flat", [P, (2 * C2 - 1) * E + P], F32R)
        wg_sb = wg_flat[:, 0:2 * C2 * E].rearrange("p (a c e) -> p a c e", a=2, c=C2)
        bias = sb("bias", [P, NBCOL], F32)
        rows = sb("rows", [P, 3, D], F32)
        b2_stack = sb("b2_stack", [3 * E, D], F32R)
        wexp_stack = sb("wexp_stack", [3 * E, S], F32R)
        wexp_parts = sb("wexp_parts", [P, 2, 3 * E], F32R)
        cst = sb("cst", [P, NCONST], F32)
        stack = {c: sb(f"stack{c}", [P, HALF, 2, S], F32R) for c in "AB"}
        staging = sb("staging", [P, 4, C2, S], F32R)
        val = {c: sb(f"val{c}", [P, 2, H, 2 * HD], F32) for c in "AB"}
        act_t = sb("act_t", [P, 2, C2, S], F32R)
        h_t = sb("h_t", [P, 2, C2, S], F32R)
        o_t = sb("o_t", [P, 2, C2, S], F32R)
        ctx_raw = sb("ctx_raw", [P, C2, S], F32)
        prob = sb("prob", [P, HALF, 2 * S], F32)
        hid = sb("hid", [P, 2, 2, C2, S], F32R)
        relu = sb("relu", [P, 2, C2, S], F32)
        heads = sb("heads", [P, 8, S], F32)
        o_tok = heads[:, 4:6, :]
        res2 = heads[:, 6:8, :]
        x_in = sb("x_in", [P, 2, D], F32)
        x_res = sb("x_res", [P, 2, D], F32)
        acc = sb("acc", [P, 2, D], F32)
        mx = {c: sb(f"mx{c}", [P, 2, H], F32) for c in "AB"}
        mrow = sb("mrow", [HALF, S], F32R)
        rden = sb("rden", [P, H], F32)
        stats = sb("stats", [P, 2, 6], F32)
        mv = sb("mv", [P, 2, 2], F32)
        rstd = sb("rstd", [P, 2], F32)
        gate = sb("gate", [P, 2, E], F32)
        top = sb("top", [P, 2, E], F32)
        top_at = sb("top_at", [P, 2, E], U32)
        top_f = sb("top_f", [P, 2, E], F32)
        first = sb("first", [P, 2, E], F32)
        second = sb("second", [P, 2, E], F32)
        wexp = sb("wexp", [P, 2, E], F32)
        gate_t = sb("gate_t", [E, S], F32)
        normed = prob

        def bank(name):
            return ctx.enter_context(nc.psum_tensor(name, [P, 512], F32))

        s_bank = [bank(f"s_bank{n}") for n in range(2)]
        t_bank = [bank(f"t_bank{n}") for n in range(2)]
        o_bank = bank("o_bank")
        g_bank = [bank(f"g_bank{n}") for n in range(3)]

        raw_in = [sem(f"raw_in{n}") for n in range(4)]
        first_in = sem("first_in")
        small_in = sem("small_in")
        raw_hi = sem("raw_hi")
        raw_lo = sem("raw_lo")
        fold_done = sem("fold_done")
        folded_hi = sem("folded_hi")
        folded = sem("folded")
        ones_set = sem("ones_set")
        wg_split = sem("wg_split")
        b2_split = sem("b2_split")
        b2_ready = sem("b2_ready")
        x_loaded = sem("x_loaded")
        res_loaded = sem("res_loaded")
        ctx_loaded = sem("ctx_loaded")
        out_stored = sem("out_stored")
        ln1 = sem("ln1")
        ln2 = sem("ln2")
        ctx_split = sem("ctx_split")
        res_ready = sem("res_ready")
        acc_ready = sem("acc_ready")
        y_added = sem("y_added")
        gate_step = sem("gate_step")
        relu_done = sem("relu_done")
        hid_hi = sem("hid_hi")
        hid_lo = sem("hid_lo")
        filled = {(c, n): sem(f"filled{c}{n}") for c in "AB" for n in range(2)}
        s_done = {c: sem(f"s_done{c}") for c in "AB"}
        max_done = {c: sem(f"max_done{c}") for c in "AB"}
        mrow_in = {(c, n): sem(f"mrow_in{c}{n}") for c in "AB" for n in range(2)}
        st_done = {c: sem(f"st_done{c}") for c in "AB"}
        exp_done = {c: sem(f"exp_done{c}") for c in "AB"}
        masked = sem("masked")
        av_done = {c: sem(f"av_done{c}") for c in "AB"}
        heads_out = {c: sem(f"heads_out{c}") for c in "AB"}
        inverted = {c: sem(f"inverted{c}") for c in "AB"}
        done = {n: sem(f"{n}_done") for n in NAMES}
        high = {n: sem(f"{n}_high") for n in ("xt", "ht", "q1", "k1", "q2", "k2", "otA", "otB")}
        read = {n: sem(f"{n}_read") for n in NAMES}

        y_order = [(name, number) for off in (-2, -3) for _, _, _, name, o, number in JOBS
                   if o == off and name in ("w2", "bw")]
        y_place = {y: n + 1 for n, y in enumerate(y_order)}

        def count(name, p, number):
            return per(name) * p[0] + (number + 1)

        passed = sem("passed")

        def alone(engine):
            engine.sem_inc(passed, 1)

        block = ctx.enter_context(nc.Block())
        RAW = [("att", WQ1), ("att", WK1), ("att", WV1), ("att", WK2), ("att", WV2), ("att", WO2)]
        ATT = len(RAW)
        RAW += [(m, e) for e in range(E) for m in ("up", "down")]

        FIRST_USE = ("q1", "k1", "v1", "k2", "v2", "wo")
        RAW_STEPS = {(0, 1): (2, 3), (0, 9): (4, 5)}
        for i, n in enumerate(range(ATT, len(RAW))):
            RAW_STEPS[(0, 10 + i) if i < 6 else (1, i - 6)] = (n,)
        FOLD = (0, 9)

        def raw_slot(n):
            return heads[:, 2 * (n % 4):2 * (n % 4) + 2, :]

        def split_to(kind, i, part):
            return {"att": w_att, "up": w_up, "down": w_down}[kind][:, i, part, :, :]

        @block.sync
        def _(sp):
            sp.dma_start(x_in[:], x[0].rearrange("(t p) d -> p t d", p=P)).then_inc(x_loaded, DMA_INC)
            sp.dma_start(cst[:], const).then_inc(first_in, DMA_INC)
            sp.dma_start(bias[:], bcol).then_inc(first_in, DMA_INC)
            def load_raw(n):
                kind, i = RAW[n]
                src = {"att": watt, "up": w1, "down": w2}[kind][i]
                if n >= 4:
                    sp.wait_ge(raw_lo, n - 3)
                sp.dma_start(raw_slot(n), src.rearrange("(c p) n -> p c n", p=P)).then_inc(raw_in[n % 4], DMA_INC)

            for n in range(4):
                load_raw(n)
            sp.dma_start(rows[:], brow.partition_broadcast(P)).then_inc(small_in, DMA_INC)
            sp.dma_start(relu[:, 0], watt[7].rearrange("(c p) n -> p c n", p=P)).then_inc(small_in, DMA_INC)
            sp.dma_start(acc[:], watt[WQO].rearrange("(c p) n -> p c n", p=P)).then_inc(small_in, DMA_INC)
            for k in range(3):
                sp.dma_start(x_res[E * k:E * (k + 1), 0, :], b2).then_inc(small_in, DMA_INC)
            sp.dma_start(wg_raw[:], wg.rearrange("(c p) e -> p c e", p=P)).then_inc(small_in, DMA_INC)
            sp.dma_start(ctx_raw[:], ctxT[0].rearrange("(c p) s -> p c s", p=P)).then_inc(ctx_loaded, DMA_INC)
            for n in range(4, ATT + 2):
                load_raw(n)
            sp.wait_ge(ones_set, 4)

            def fill(layer, p, half):
                for name in ("q1", "k1") if layer == "A" else ("q2", "k2"):
                    sp.wait_ge(read[name], p[0] + 1)
                if exists(at(p, -1)):
                    sp.wait_ge(st_done[layer], H * p[0] - HALF * (1 - half))
                for c in range(2):
                    for r, (q, k) in enumerate(BLOCKS):
                        low = (P // 2) * c + HD * r
                        sp.dma_start(
                            stack[layer][low:low + HD, 4 * half:4 * half + 4, :, :].bitcast(F32),
                            staging[(P // 2) * c:(P // 2) * (c + 1), q:k + 1:k - q, half, :].bitcast(F32),
                        ).then_inc(filled[layer, half], DMA_INC)

            def maxima(layer, p, half):
                sp.wait_ge(read["mt" + layer], 2 * p[0] + half + 1)
                sp.dma_start(stack[layer][STACK:STACK + P // 2 + 1:P // 2, 4 * half:4 * half + 4, 0, :].bitcast(F32),
                             mrow[:].bitcast(F32)).then_inc(mrow_in[layer, half], DMA_INC)

            def body(j):
                a, b, nxt, old, oldest = (at(j, k) for k in (0, -1, 1, -2, -3))
                if j[1] == 0:
                    sp.wait_ge(b2_split, 2)
                    sp.dma_start(b2_stack[E:2 * E, :].bitcast(F32), x_res[E:2 * E, 1, :]).then_inc(b2_ready, DMA_INC)
                    sp.wait_ge(b2_ready, DMA_INC)
                if exists(b):
                    fill("B", b, 1)
                if exists(a):
                    maxima("A", a, 1)
                if exists(at(j, 2)):
                    sp.wait_ge(done["xt"], j[0] + 2)
                    alone(sp)
                    sp.dma_start(x_in[:], x[j[0] + 2].rearrange("(t p) d -> p t d", p=P)).then_inc(x_loaded, DMA_INC)
                if exists(nxt):
                    fill("A", nxt, 0)
                if j[1] == -1:
                    for n in range(ATT + 2, ATT + 8):
                        load_raw(n)
                if exists(b):
                    maxima("B", b, 0)
                if exists(oldest):
                    sp.wait_ge(y_added, (E + 1) * (oldest[0] + 1))
                    alone(sp)
                    sp.dma_start(out[oldest[0]].rearrange("(t p) d -> p t d", p=P), acc[:]).then_inc(out_stored, DMA_INC)
                if exists(b):
                    if exists(old):
                        sp.wait_ge(done["ht"], old[0] + 1)
                    alone(sp)
                    sp.dma_start(x_res[:], x[b[0]].rearrange("(t p) d -> p t d", p=P)).then_inc(res_loaded, DMA_INC)
                if exists(nxt):
                    fill("A", nxt, 1)
                if j[1] == -1:
                    for n in range(ATT + 8, len(RAW)):
                        load_raw(n)
                if exists(b):
                    maxima("B", b, 1)
                if exists(nxt) and exists(a):
                    sp.wait_ge(ctx_split, 2 * (a[0] + 1))
                    alone(sp)
                    sp.dma_start(ctx_raw[:], ctxT[nxt[0]].rearrange("(c p) s -> p c s", p=P)).then_inc(ctx_loaded, DMA_INC)
                if exists(a):
                    fill("B", a, 0)
                if exists(nxt):
                    maxima("A", nxt, 0)
                if j[1] == -1:
                    sp.wait_ge(raw_lo, len(RAW))

            iterations(nc.sync, body)
            sp.wait_ge(out_stored, DMA_INC * B)

        @block.gpsimd
        def _(pool):
            def root(counter, p):
                pool.wait_ge(counter, 8 * p[0] + 5)
                nc.gpsimd.tensor_tensor(rstd[:], rstd[:], cst[:, POWER:POWER + 2], ALU.pow).then_inc(counter, 1)

            pool.wait_ge(first_in, FIRST * DMA_INC)
            root(ln1, (0, 0))
            for c in "AB":
                nc.gpsimd.memset(val[c][:], 1.0).then_inc(ones_set, 1)
                nc.gpsimd.memset(stack[c][:, :, :, :].bitcast(F32), -1.0).then_inc(ones_set, 1)
            nc.gpsimd.memset(wg_flat[:].bitcast(F32), 0.0).then_inc(wg_split, 1)
            pool.wait_ge(small_in, SMALL * DMA_INC)
            pool.wait_ge(wg_split, 1)
            nc.gpsimd.tensor_copy(wg_sb[:, HI], wg_raw[:]).then_inc(wg_split, 1)
            pool.wait_ge(wg_split, 2)
            nc.gpsimd.tensor_tensor(wg_sb[:, LO], wg_raw[:], wg_sb[:, HI], ALU.subtract).then_inc(wg_split, 1)
            nc.gpsimd.tensor_copy(b2_stack[:], x_res[0:3 * E, 0, :]).then_inc(b2_split, 1)
            pool.wait_ge(b2_split, 1)
            nc.gpsimd.tensor_tensor(x_res[0:3 * E, 1, :], x_res[0:3 * E, 0, :], b2_stack[:], ALU.subtract) \
                .then_inc(b2_split, 1)

            def split_context(p):
                pool.wait_ge(ctx_loaded, DMA_INC * (p[0] + 1))
                v1 = at(p, 1) if exists(at(p, 1)) else p
                pool.wait_ge(done["v1"], v1[0] + 1)
                if exists(at(p, -1)):
                    pool.wait_ge(done["v2"], p[0])
                alone(pool)
                nc.gpsimd.tensor_copy(act_t[:, HI], ctx_raw[:]).then_inc(ctx_split, 1)
                pool.wait_ge(ctx_split, 2 * p[0] + 1)
                nc.gpsimd.tensor_tensor(act_t[:, LO], ctx_raw[:], act_t[:, HI], ALU.subtract).then_inc(ctx_split, 1)

            def body(j):
                a, b, nxt, old = (at(j, k) for k in (0, -1, 1, -2))
                for slot in range(2):
                    for step in range(H):
                        if (slot, step) == (1, 15) and exists(at(j, 2)):
                            root(ln1, at(j, 2))
                        if (slot, step) == (0, 8) and exists(old):
                            root(ln2, old)
                        if slot == 0 and exists(a):
                            pool.wait_ge(exp_done["A"], H * a[0] + step + 1)
                            diagonal = prob[:, step % HALF, P:3 * P].rearrange("p (b q) -> p b q", b=2)
                            alone(pool)
                            nc.gpsimd.affine_select(out=diagonal, in_=diagonal, compare_op=ALU.is_ge, fill=0.0, base=0,
                                                    pattern=[[0, 2], [1, P]], channel_multiplier=-1).then_inc(masked, 1)
                        for n, name, p, number in steps_of(slot, step, j):
                            if name == "w1":
                                pool.wait_ge(hid_hi, count("w1", p, number))
                                nc.gpsimd.tensor_tensor(hid[:, number % 2, LO], relu[:, number % 2], hid[:, number % 2, HI],
                                                        ALU.subtract).then_inc(hid_lo, 1)
                        if (slot, step) == (0, 0) and exists(old):
                            pool.wait_ge(res_loaded, DMA_INC * (old[0] + 1))
                            for t in range(2):
                                nc.gpsimd.tensor_tensor(x_res[:, t], x_res[:, t], rows[:, 2], ALU.add).then_inc(res_ready, 1)
                        if (slot, step) == (1, 3) and exists(a):
                            split_context(a)

            iterations(nc.gpsimd, body)

        def mrow_free(engine, name, p, number):
            c = name[-1]
            if number == 1:
                engine.wait_ge(mrow_in[c, 0], DMA_INC * (p[0] + 1))
            else:
                before = unit_before(c, p)
                if before:
                    engine.wait_ge(mrow_in[before[0], 1], DMA_INC * (before[1][0] + 1))

        def o_t_free(engine, layer, p):
            if layer == "A":
                if exists(at(p, -2)):
                    engine.wait_ge(done["wo"], p[0] - 1)
                elif exists(at(p, -1)):
                    engine.wait_ge(done["q2"], p[0])
            elif exists(at(p, 1)):
                engine.wait_ge(done["q2"], p[0] + 2)
            else:
                engine.wait_ge(done["wo"], p[0])

        def staging_free(engine, name, p):
            before = unit_before("A" if name[-1] == "1" else "B", p)
            if before:
                for half in range(2):
                    engine.wait_ge(filled[before[0], half], FILL_DMAS * DMA_INC * (before[1][0] + 1))

        @block.scalar
        def _(act):
            act.wait_ge(first_in, FIRST * DMA_INC)

            def raw_high(n):
                kind, i = RAW[n]
                act.wait_ge(raw_in[n % 4], DMA_INC * (n // 4 + 1))
                nc.scalar.activation(split_to(kind, i, HI), raw_slot(n), ACT.Copy).then_inc(raw_hi, 1)

            for n in range(2):
                raw_high(n)

            def fold_high():
                act.wait_ge(fold_done, 1)
                nc.scalar.activation(w_att[:, WQO, HI, :, :], g_bank[0][:, :].rearrange("p (c n) -> p c n", c=C2), ACT.Copy) \
                    .then_inc(folded_hi, 1)

            def exponent(layer, p, h):
                act.wait_ge(st_done[layer], H * p[0] + h + 1)
                if h >= HALF:
                    act.wait_ge(av_done[layer], 4 * p[0] + h // 4 - 1)
                else:
                    before = unit_before(layer, p)
                    if before:
                        act.wait_ge(av_done[before[0]], 4 * before[1][0] + 3 + h // 4)
                low = P if layer == "A" else 0
                nc.scalar.activation(prob[:, h % HALF, low:], t_bank[h % 2][:, low:], ACT.Exp, scale=HD ** -0.5) \
                    .then_inc(exp_done[layer], 1)

            def heads_copy(layer, p, half):
                act.wait_ge(av_done[layer], 4 * p[0] + 2 * half + 2)
                before = unit_before(layer, p)
                if before:
                    act.wait_ge(done["hd" + before[0]], 2 * before[1][0] + half + 1)
                nc.scalar.activation(heads[:, 2 * half:2 * half + 2, :],
                                     o_bank[:, :].rearrange("p (g q) -> p g q", g=2), ACT.Copy) \
                    .then_inc(heads_out[layer], 1)

            def evacuate(n, name, p, number):
                g = g_bank[JOBS[n][2]][:, :].rearrange("p (c s) -> p c s", c=2)
                if name not in high and name not in ("w1", "mtA", "mtB", "gate"):
                    return
                act.wait_ge(done[name], count(name, p, number))
                if name in ("xt", "ht"):
                    if name == "xt" and exists(at(p, -2)):
                        act.wait_ge(done["v2"], p[0] - 1)
                    elif name == "xt" and exists(at(p, -1)):
                        act.wait_ge(done["v1"], p[0])
                    if name == "ht" and exists(at(p, -1)):
                        act.wait_ge(done["w1"], E * p[0])
                    nc.scalar.activation((act_t if name == "xt" else h_t)[:, HI], g, ACT.Copy).then_inc(high[name], 1)
                elif name == "gate":
                    if exists(at(p, -1)):
                        act.wait_ge(done["gt"], p[0])
                    nc.scalar.activation(gate_t[:], g_bank[JOBS[n][2]][0:E, 0:S], ACT.Identity, bias=bias[0:E, BG:BG + 1]) \
                        .then_inc(read["gate"], 1)
                elif name in ("mtA", "mtB"):
                    mrow_free(act, name, p, number)
                    nc.scalar.activation(mrow[:], g_bank[JOBS[n][2]][0:HALF, 0:S], ACT.Copy).then_inc(read[name], 1)
                elif name in ("otA", "otB"):
                    o_t_free(act, name[-1], p)
                    nc.scalar.activation(o_t[:, HI, number, :], g[:, 0, :], ACT.Copy).then_inc(high[name], 1)
                elif name == "w1":
                    if number >= 2 or exists(at(p, -1)):
                        act.wait_ge(hid_lo, E * p[0] + number - 1)
                    for c in range(C2):
                        nc.scalar.activation(relu[:, number % 2, c, :], g[:, c, :], ACT.Relu,
                                             bias=bias[:, B1 + 2 * number + c:B1 + 2 * number + c + 1]).then_inc(relu_done, 1)
                else:
                    col, place = {"q1": (BQ1, QHI), "k1": (BK1, KHI), "q2": (BQ2, QHI), "k2": (BK2, KHI)}[name]
                    staging_free(act, name, p)
                    for c in range(C2):
                        nc.scalar.activation(staging[:, place, c, :], g[:, c, :], ACT.Identity,
                                             bias=bias[:, col + c:col + c + 1]).then_inc(high[name], 1)

            def hidden_high(p, number):
                act.wait_ge(relu_done, 2 * count("w1", p, number))
                if number >= 2 or exists(at(p, -1)):
                    act.wait_ge(done["w2"], E * p[0] + number - 1)
                nc.scalar.activation(hid[:, number % 2, HI], relu[:, number % 2], ACT.Copy).then_inc(hid_hi, 1)

            def body(j):
                a, b, nxt, old = (at(j, k) for k in (0, -1, 1, -2))
                for slot in range(2):
                    layer, p = ("A", a) if slot == 0 else ("B", b)
                    for step in range(H):
                        if exists(p):
                            exponent(layer, p, step)
                        for job in steps_of(slot, step, j):
                            evacuate(*job)
                        for _, name, p1, number in jobs_before(slot, step, j):
                            if name == "w1":
                                hidden_high(p1, number)
                        if j[1] == -1:
                            for n in RAW_STEPS.get((slot, step), ()):
                                raw_high(n)
                            if (slot, step) == FOLD:
                                fold_high()
                        if (slot, step) == (0, 1) and exists(old):
                            heads_copy("B", old, 1)
                        if (slot, step) == (0, 9) and exists(a):
                            heads_copy("A", a, 0)
                        if (slot, step) == (1, 1) and exists(a):
                            heads_copy("A", a, 1)
                        if (slot, step) == (1, 9) and exists(b):
                            heads_copy("B", b, 0)

            iterations(nc.scalar, body)

        @block.vector
        def _(dve):
            dve.wait_ge(first_in, FIRST * DMA_INC)

            def raw_low(n):
                kind, i = RAW[n]
                dve.wait_ge(raw_hi, n + 1)
                nc.vector.tensor_tensor(split_to(kind, i, LO), raw_slot(n), split_to(kind, i, HI), ALU.subtract) \
                    .then_inc(raw_lo, 1)

            def fold_low():
                dve.wait_ge(folded_hi, 1)
                nc.vector.tensor_tensor(w_att[:, WQO, LO, :, :], g_bank[0][:, :].rearrange("p (c n) -> p c n", c=C2),
                                        w_att[:, WQO, HI, :, :], ALU.subtract).then_inc(folded, 1)
                dve.wait_ge(fold_done, 2)
                nc.vector.tensor_tensor(bias[:, BQ2:BQ2 + 2], g_bank[1][:, 0:2], bias[:, BQ2:BQ2 + 2], ALU.add) \
                    .then_inc(folded, 1)

            def ln_stats(src, counter, p):
                for t in range(2):
                    nc.vector.bn_stats(stats[:, t, :], src[:, t, :]).then_inc(counter, 1)

            def ln_variance(counter, p):
                dve.wait_ge(counter, 8 * p[0] + 2)
                alone(dve)
                for t in range(2):
                    nc.vector.bn_aggr(mv[:, t, :], stats[:, t, :]).then_inc(counter, 1)
                dve.wait_ge(counter, 8 * p[0] + 4)
                nc.vector.tensor_scalar(rstd[:, :], mv[:, :, 1], EPS, None, ALU.add).then_inc(counter, 1)

            def ln_normalise(src, dst, counter, p):
                dve.wait_ge(counter, 8 * p[0] + 6)
                for t in range(2):
                    nc.vector.tensor_scalar(dst[:, t, :], src[:, t, :], mv[:, t, 0:1], rstd[:, t:t + 1],
                                            ALU.subtract, ALU.mult).then_inc(counter, 1)

            dve.wait_ge(x_loaded, DMA_INC)
            ln_stats(x_in, ln1, (0, 0))
            ln_variance(ln1, (0, 0))
            for n in range(2):
                raw_low(n)

            def row_max(layer, p, h):
                dve.wait_ge(s_done[layer], H * p[0] + h + 1)
                if h % HALF == 0 and exists(at(p, -1)):
                    dve.wait_ge(done["mt" + layer], 2 * p[0] + h // HALF - 1)
                col = HALF * (h // HALF) + 4 * (h % 2) + h % HALF // 2
                s = s_bank[h % 2]
                if layer == "B":
                    nc.vector.tensor_reduce(mx["B"][:, :, col:col + 1], s[:, :].rearrange("p (c k) -> p c k", c=2),
                                            AX.X, ALU.max).then_inc(max_done["B"], 1)
                    return
                alone(dve)
                nc.vector.tensor_tensor_reduce(out=s[:, 0:P], in0=s[:, 0:P], in1=cst[:, CAUSAL + P:CAUSAL + 2 * P],
                                               scale=1.0, scalar=-3e38, op0=ALU.add, op1=ALU.max,
                                               accum_out=mx["A"][:, 0, col:col + 1])
                nc.vector.tensor_tensor_reduce(out=s[:, S:2 * S], in0=s[:, S:2 * S], in1=cst[:, CAUSAL:CAUSAL + 2 * P],
                                               scale=1.0, scalar=-3e38, op0=ALU.add, op1=ALU.max,
                                               accum_out=mx["A"][:, 1, col:col + 1]).then_inc(max_done["A"], 1)

            def evacuate(n, name, p, number):
                g = g_bank[JOBS[n][2]][:, :].rearrange("p (c s) -> p c s", c=2)
                if name in ("w1", "mtA", "mtB", "gate"):
                    return
                dve.wait_ge(done[name], count(name, p, number))
                if name in ("xt", "ht"):
                    dve.wait_ge(high[name], p[0] + 1)
                    t = act_t if name == "xt" else h_t
                    nc.vector.tensor_tensor(t[:, LO], g, t[:, HI], ALU.subtract).then_inc(read[name], 1)
                elif name in ("hdA", "hdB"):
                    layer = name[-1]
                    pairs = g_bank[JOBS[n][2]][:, :].rearrange("p (h e) -> p h e", h=H)
                    nc.vector.reciprocal(rden[:, :].rearrange("p (h e) -> p h e", e=1), pairs[:, :, HD:HD + 1]) \
                        .then_inc(inverted[layer], 1)
                    before = unit_before(layer, p)
                    if before:
                        dve.wait_ge(done["ot" + before[0]], 2 * before[1][0] + number + 1)
                    dve.wait_ge(inverted[layer], count(name, p, number))
                    nc.vector.tensor_tensor(o_tok[:, number, :].rearrange("p (h e) -> p h e", h=H), pairs[:, :, 0:HD],
                                            rden[:, :].rearrange("p (h e) -> p h e", e=1).to_broadcast([P, H, HD]),
                                            ALU.mult).then_inc(read[name], 1)
                elif name in ("otA", "otB"):
                    dve.wait_ge(high[name], count(name, p, number))
                    nc.vector.tensor_tensor(o_t[:, LO, number, :], g[:, 0, :], o_t[:, HI, number, :], ALU.subtract) \
                        .then_inc(read[name], 1)
                elif name in ("v1", "v2"):
                    layer = "A" if name == "v1" else "B"
                    if p[1] == 0:
                        dve.wait_ge(small_in, SMALL * DMA_INC)
                        dve.wait_ge(ones_set, 4)
                    if exists(at(p, -1)):
                        dve.wait_ge(av_done[layer], 4 * p[0])
                    for t in range(2):
                        ins = nc.vector.tensor_tensor(val[layer][:, t, :, 0:HD],
                                                      g[:, t, :].rearrange("p (h e) -> p h e", h=H),
                                                      rows[:, 0 if layer == "A" else 1, :].rearrange("p (h e) -> p h e", h=H),
                                                      ALU.add)
                    ins.then_inc(read[name], 1)
                elif name == "wo":
                    dve.wait_ge(res_ready, 2 * (p[0] + 1))
                    nc.vector.tensor_tensor(res2, g, x_res[:], ALU.add).then_inc(read["wo"], 1)
                    dve.wait_ge(read["wo"], p[0] + 1)
                    ln_stats(res2, ln2, p)
                elif name == "gt":
                    gating(n, p)
                elif name == "wt":
                    if exists(at(p, -1)):
                        dve.wait_ge(done["bw"], p[0])
                    nc.vector.tensor_copy(wexp_stack[:], g_bank[JOBS[n][2]][0:3 * E, 0:S]).then_inc(read["wt"], 1)
                elif name == "bw":
                    order = y_order.index(("bw", 0))
                    dve.wait_ge(y_added, (E + 1) * p[0] + order)
                    nc.vector.tensor_tensor(acc[:], g, acc[:], ALU.add).then_inc(y_added, 1)
                elif name == "w2":
                    order = y_order.index(("w2", number))
                    if order or exists(at(p, -1)):
                        dve.wait_ge(y_added, (E + 1) * p[0] + order)
                    if order == 0 and exists(at(p, -1)):
                        dve.wait_ge(out_stored, DMA_INC * p[0])
                    for t in range(2):
                        ins = nc.vector.scalar_tensor_tensor(out=acc[:, t, :], in0=g[:, t, :],
                                                             scalar=wexp[:, t, number:number + 1],
                                                             in1=(acc if order else res2)[:, t, :],
                                                             op0=ALU.mult, op1=ALU.add)
                    ins.then_inc(y_added, 1)
                else:
                    col, hi, lo = {"q1": (BQ1, QHI, QLO), "k1": (BK1, KHI, KLO),
                                   "q2": (BQ2, QHI, QLO), "k2": (BK2, KHI, KLO)}[name]
                    dve.wait_ge(high[name], 2 * (p[0] + 1))
                    for c in range(C2):
                        ins = nc.vector.scalar_tensor_tensor(out=staging[:, lo, c, :], in0=g[:, c, :],
                                                             scalar=bias[:, col + c:col + c + 1], in1=staging[:, hi, c, :],
                                                             op0=ALU.add, op1=ALU.subtract)
                    ins.then_inc(read[name], 1)

            def gating(n, p):
                base = GATE_STEPS * p[0]
                nc.vector.tensor_copy(gate[:].rearrange("p t e -> p (t e)"), g_bank[JOBS[n][2]][:, 0:2 * E]).then_inc(read["gt"], 1)
                dve.wait_ge(read["gt"], p[0] + 1)
                alone(dve)
                for t in range(2):
                    nc.vector.max(top[:, t, :], gate[:, t, :]).then_inc(gate_step, 1)
                dve.wait_ge(gate_step, base + 2)
                alone(dve)
                for t in range(2):
                    nc.vector.max_index(top_at[:, t, :], top[:, t, :], gate[:, t, :]).then_inc(gate_step, 1)

            def gate_choice(p):
                base = GATE_STEPS * p[0]
                dve.wait_ge(gate_step, base + 4)
                nc.vector.tensor_copy(top_f[:], top_at[:]).then_inc(gate_step, 1)
                dve.wait_ge(gate_step, base + 5)
                for t in range(2):
                    for k, place in enumerate((first, second)):
                        ins = nc.vector.tensor_scalar(place[:, t, :], cst[:, EXPERTS:EXPERTS + E], top_f[:, t, k:k + 1],
                                                      top[:, t, k:k + 1], ALU.is_equal, ALU.mult)
                ins.then_inc(gate_step, 1)
                dve.wait_ge(gate_step, base + 6)
                nc.vector.tensor_tensor(wexp[:], first[:], second[:], ALU.add).then_inc(gate_step, 1)
                dve.wait_ge(gate_step, base + 7)
                for k in range(2):
                    nc.vector.tensor_copy(wexp_parts[:, :, E * k:E * (k + 1)], wexp[:]).then_inc(gate_step, 1)
                dve.wait_ge(gate_step, base + 9)
                nc.vector.tensor_tensor(wexp_parts[:, :, 2 * E:3 * E], wexp[:], wexp_parts[:, :, 0:E], ALU.subtract) \
                    .then_inc(gate_step, 1)

            def body(j):
                a, b, nxt, old = (at(j, k) for k in (0, -1, 1, -2))
                for slot in range(2):
                    layer, p = ("B", b) if slot == 0 else ("A", nxt)
                    for step in range(H):
                        if exists(p):
                            row_max(layer, p, step)
                        if (slot, step) == (1, 14) and exists(at(j, 2)):
                            dve.wait_ge(x_loaded, DMA_INC * (j[0] + 3))
                            ln_stats(x_in, ln1, at(j, 2))
                        if (slot, step) == (1, 15) and exists(at(j, 2)):
                            ln_variance(ln1, at(j, 2))
                        if (slot, step) == (0, 0) and exists(nxt):
                            ln_normalise(x_in, x_in, ln1, nxt)
                        if (slot, step) == (0, 8) and exists(old):
                            ln_variance(ln2, old)
                        if (slot, step) == (0, 9) and exists(old):
                            ln_normalise(res2, x_res, ln2, old)
                        if (slot, step) == (0, 15) and exists(old):
                            gate_choice(old)
                        for late in (True, False):
                            for job in jobs_before(slot, step, j) if late else steps_of(slot, step, j):
                                if (job[1] in ("q1", "k1", "q2", "k2")) == late:
                                    evacuate(*job)
                        if j[1] == -1:
                            for n in RAW_STEPS.get((slot, step), ()):
                                raw_low(n)
                            if (slot, step) == FOLD:
                                fold_low()

            iterations(nc.vector, body)

        @block.tensor
        def _(pe):
            pe.wait_ge(first_in, FIRST * DMA_INC)

            def fold():
                pe.wait_ge(small_in, SMALL * DMA_INC)
                for name in ("xt", "q1", "k1"):
                    pe.wait_ge(read[name], 1)
                for o in range(C2):
                    for c in range(C2):
                        last = nc.tensor.matmul(g_bank[0][:, o * D:(o + 1) * D], relu[:, 0, c, o * P:(o + 1) * P],
                                                acc[:, c, :], start=(c == 0), stop=(c == C2 - 1))
                last.then_inc(fold_done, 1)
                for o in range(C2):
                    for c in range(C2):
                        last = nc.tensor.matmul(g_bank[1][:, o:o + 1], acc[:, c, o * P:(o + 1) * P],
                                                bias[:, BO1 + c:BO1 + c + 1], start=(c == 0), stop=(c == C2 - 1))
                last.then_inc(fold_done, 1)
                pe.wait_ge(folded, 2)

            def product(g, weights, data, weights_stay):
                still, moving = (weights, data) if weights_stay else (data, weights)
                for o in range(2):
                    for c in range(C2):
                        for a, b in ((HI, HI), (HI, LO), (LO, HI)):
                            last = nc.tensor.matmul(g[:, o * D:(o + 1) * D], still[:, a, c, o * P:(o + 1) * P],
                                                    moving[:, b, c, :], start=(c == 0 and a == b),
                                                    stop=(c == C2 - 1 and a == LO))
                return last

            def transpose_chunks(g, data):
                for t in range(2):
                    for c in range(C2):
                        last = nc.tensor.transpose(g[:, c * S + t * P:c * S + (t + 1) * P],
                                                   data[:, t, c * P:(c + 1) * P], cst[:, IDENT:IDENT + P])
                return last

            def job(n, name, p, number, j):
                g = g_bank[JOBS[n][2]]
                before = job_before(n, j)
                if before:
                    name0, p0, number0 = before
                    if name0 == "w1":
                        pe.wait_ge(relu_done, 2 * count("w1", p0, number0))
                    elif name0 in ("w2", "bw"):
                        pe.wait_ge(y_added, (E + 1) * p0[0] + y_place[(name0, number0)])
                    else:
                        pe.wait_ge(read[name0], count(name0, p0, number0))
                if p[1] == 0 and name in FIRST_USE:
                    pe.wait_ge(raw_lo, FIRST_USE.index(name) + 1)
                if name == "xt":
                    pe.wait_ge(ln1, 8 * (p[0] + 1))
                    last = transpose_chunks(g, x_in)
                elif name == "ht":
                    pe.wait_ge(ln2, 8 * (p[0] + 1))
                    last = transpose_chunks(g, x_res)
                elif name in ("q1", "k1"):
                    pe.wait_ge(read["xt"], p[0] + 1)
                    last = product(g, w_att[:, WQ1 if name == "q1" else WK1], act_t, True)
                elif name == "v1":
                    pe.wait_ge(read["xt"], p[0] + 1)
                    last = product(g, w_att[:, WV1], act_t, False)
                elif name == "k2":
                    pe.wait_ge(ctx_split, 2 * (p[0] + 1))
                    last = product(g, w_att[:, WK2], act_t, True)
                elif name == "v2":
                    pe.wait_ge(ctx_split, 2 * (p[0] + 1))
                    last = product(g, w_att[:, WV2], act_t, False)
                elif name == "q2":
                    pe.wait_ge(read["otA"], 2 * (p[0] + 1))
                    last = product(g, w_att[:, WQO], o_t, True)
                elif name == "wo":
                    pe.wait_ge(read["otB"], 2 * (p[0] + 1))
                    last = product(g, w_att[:, WO2], o_t, False)
                elif name == "gate":
                    pe.wait_ge(read["ht"], p[0] + 1)
                    if p[1] == 0:
                        pe.wait_ge(wg_split, 3)
                    for c in range(C2):
                        for a, b in ((HI, HI), (HI, LO), (LO, HI)):
                            last = nc.tensor.matmul(g[:, 0:S], wg_flat[:, (C2 * a + c) * E:(C2 * a + c) * E + P],
                                                    h_t[:, b, c, :], start=(c == 0 and a == b), stop=(c == C2 - 1 and a == LO))
                elif name == "gt":
                    pe.wait_ge(read["gate"], p[0] + 1)
                    for t in range(2):
                        last = nc.tensor.matmul(g[:, t * E:(t + 1) * E], gate_t[:, t * P:(t + 1) * P],
                                                cst[0:E, IDENT:IDENT + E], start=True, stop=True)
                elif name == "w1":
                    pe.wait_ge(read["ht"], p[0] + 1)
                    if p[1] == 0:
                        pe.wait_ge(raw_lo, ATT + 2 * number + 1)
                    last = product(g, w_up[:, number], h_t, True)
                elif name == "w2":
                    pe.wait_ge(hid_lo, count("w2", p, number))
                    if p[1] == 0:
                        pe.wait_ge(raw_lo, ATT + 2 * number + 2)
                    last = product(g, w_down[:, number], hid[:, number % 2], False)
                elif name in ("hdA", "hdB"):
                    pe.wait_ge(heads_out[name[-1]], count(name, p, number))
                    for t in range(2):
                        for k in range(2):
                            last = nc.tensor.transpose(g[:, (2 * t + k) * P:(2 * t + k + 1) * P],
                                                       heads[:, 2 * number + k, t * P:(t + 1) * P],
                                                       cst[:, IDENT:IDENT + P])
                elif name in ("otA", "otB"):
                    pe.wait_ge(read["hd" + name[-1]], count(name, p, number))
                    for t in range(2):
                        last = nc.tensor.transpose(g[:, t * P:(t + 1) * P], o_tok[:, number, t * P:(t + 1) * P],
                                                   cst[:, IDENT:IDENT + P])
                elif name == "wt":
                    pe.wait_ge(gate_step, GATE_STEPS * (p[0] + 1))
                    for t in range(2):
                        last = nc.tensor.transpose(g[0:3 * E, t * P:(t + 1) * P], wexp_parts[:, t, :].bitcast(F32),
                                                   cst[:, IDENT:IDENT + P])
                elif name == "bw":
                    pe.wait_ge(read["wt"], p[0] + 1)
                    if p[1] == 0:
                        pe.wait_ge(b2_ready, DMA_INC)
                    for t in range(2):
                        last = nc.tensor.matmul(g[:, t * D:(t + 1) * D], wexp_stack[:, t * P:(t + 1) * P], b2_stack[:],
                                                start=True, stop=True)
                else:
                    layer = name[-1]
                    pe.wait_ge(max_done[layer], H * p[0] + HALF * (number + 1))
                    for t in range(2):
                        last = nc.tensor.transpose(g[0:HALF, t * P:(t + 1) * P],
                                                   mx[layer][:, t, HALF * number:HALF * (number + 1)],
                                                   cst[:, IDENT:IDENT + P])
                last.then_inc(done[name], 1)

            def scores(layer, p, h):
                if h % HALF == 0:
                    pe.wait_ge(filled[layer, h // HALF], FILL_DMAS * DMA_INC * (p[0] + 1))
                if h >= 2:
                    pe.wait_ge(max_done[layer], H * p[0] + h - 1)
                else:
                    before = unit_before(layer, p)
                    if before:
                        pe.wait_ge(max_done[before[0]], H * before[1][0] + H - 1 + h)
                low, qk = (P // 2) * (h % 2), stack[layer]
                for c in range(2):
                    last = nc.tensor.matmul(s_bank[h % 2][:, c * S:(c + 1) * S],
                                            qk[low:low + STACK, h // 2, 0, c * P:(c + 1) * P],
                                            qk[low:low + STACK, h // 2, 1, :], start=True, stop=True)
                last.then_inc(s_done[layer], 1)

            def shifted(layer, p, h):
                if h % HALF == 0:
                    pe.wait_ge(mrow_in[layer, h // HALF], DMA_INC * (p[0] + 1))
                if h >= 2:
                    pe.wait_ge(exp_done[layer], H * p[0] + h - 1)
                else:
                    before = unit_before(layer, p)
                    if before:
                        pe.wait_ge(exp_done[before[0]], H * before[1][0] + H - 1 + h)
                low, qk = (P // 2) * (h % 2), stack[layer]
                for c in range(2):
                    col = S * (1 - c if layer == "A" else c)
                    last = nc.tensor.matmul(t_bank[h % 2][:, col:col + S],
                                            qk[low:low + ROWS, h // 2, 1, c * P:(c + 1) * P],
                                            qk[low:low + ROWS, h // 2, 0, :], start=True, stop=True)
                last.then_inc(st_done[layer], 1)

            def values(layer, p, group):
                ready = masked if layer == "A" else exp_done["B"]
                pe.wait_ge(ready, H * p[0] + 4 * group + 4)
                if group == 0:
                    pe.wait_ge(read["v1" if layer == "A" else "v2"], p[0] + 1)
                before = unit_before(layer, p)
                if group == 0 and p[1] == 0:
                    pe.wait_ge(ones_set, 4)
                if group == 0 and before:
                    pe.wait_ge(heads_out[before[0]], 2 * before[1][0] + 2)
                if group == 2:
                    pe.wait_ge(heads_out[layer], 2 * p[0] + 1)
                o = o_bank
                base = S * (group % 2)
                for c in range(2):
                    for i in range(4):
                        h = 4 * group + i
                        if layer == "A":
                            src = prob[:, h % HALF, S:2 * S] if c == 0 else prob[:, h % HALF, P:S]
                            lo = base + P * c
                        else:
                            src = prob[:, h % HALF, S * c:S * (c + 1)]
                            lo = base
                        last = nc.tensor.matmul(o[32 * i:32 * i + 32, lo:base + S], val[layer][:, c, h, :], src,
                                                start=(c == 0), stop=(c == 1), skip_group_check=True)
                last.then_inc(av_done[layer], 1)

            def body(j):
                a, b, nxt, old = (at(j, k) for k in (0, -1, 1, -2))
                for slot in range(2):
                    s_unit = ("B", b) if slot == 0 else ("A", nxt)
                    t_unit = ("A", a) if slot == 0 else ("B", b)
                    last_unit = ("B", old) if slot == 0 else ("A", a)
                    for step in range(H):
                        if exists(s_unit[1]):
                            scores(*s_unit, step)
                        if exists(t_unit[1]):
                            shifted(*t_unit, step)
                        for n, name, p, number in steps_of(slot, step, j):
                            job(n, name, p, number, j)
                        if j[1] == -1 and (slot, step) == FOLD:
                            fold()
                        if step == 1 and exists(last_unit[1]):
                            values(*last_unit, 3)
                        if step in (5, 9, 13) and exists(t_unit[1]):
                            values(*t_unit, (step - 5) // 4)

            iterations(nc.tensor, body)


def kernel(x, ctx_1024, **w):
    import numpy as np
    import concourse.bacc as bacc
    from concourse import mybir as mb
    from concourse.bass_utils import run_bass_kernel_spmd

    def pick(name):
        return np.asarray(w["L0_" + name])

    halves, parity, elem, pair = np.meshgrid(range(2), range(2), range(HD), range(4), indexing="ij")
    order_qk = (HD * (8 * halves + 2 * pair + parity) + elem).reshape(-1)
    def flat(name):
        return pick(name).transpose(1, 0, 2).reshape(D, D)

    watt = np.stack([
        flat("xattn_Wq1")[:, order_qk], flat("xattn_Wk1")[:, order_qk], flat("xattn_Wv1"),
        flat("xattn_Wq2")[:, order_qk], flat("xattn_Wk2")[:, order_qk], flat("xattn_Wv2"),
        pick("xattn_Wo2"), pick("xattn_Wo1").T,
    ])

    def columns(v):
        return v.reshape(-1, P).T

    bcol = np.concatenate(
        [columns(pick("xattn_" + n).reshape(D)[order_qk]) for n in ("bq1", "bk1", "bq2", "bk2")]
        + [columns(pick("xattn_bo1")), columns(pick("ffn_b1")),
           np.tile(pick("ffn_b_gate"), P // E)[:, None]], axis=1)
    brow = np.stack([pick("xattn_bv1").reshape(D), pick("xattn_bv2").reshape(D), pick("xattn_bo2")])
    before = np.arange(P)[:, None] >= np.arange(P)[None, :]
    const = np.concatenate([np.eye(P), np.zeros((P, P)), np.where(before, 0.0, -1e30),
                            np.tile(np.arange(E), (P, 1)), np.full((P, 2), -0.5)], axis=1).astype(np.float32)
    arrays = {
        "x": np.asarray(x), "ctxT": np.asarray(ctx_1024).transpose(0, 2, 1), "watt": watt,
        "w1": pick("ffn_W1"), "w2": pick("ffn_W2"), "wg": pick("ffn_W_gate"), "bcol": bcol, "brow": brow,
        "b2": pick("ffn_b2"), "const": const,
    }
    arrays = {f"in_{k}": np.ascontiguousarray(v) for k, v in arrays.items()}
    nc = bacc.Bacc("TRN2", target_bir_lowering=False, num_devices=1)
    args = [nc.dram_tensor(k, v.shape, mb.dt.from_np(v.dtype), kind="ExternalInput").ap() for k, v in arrays.items()]
    out = nc.dram_tensor("out_y", (B, S, D), mb.dt.float32, kind="ExternalOutput").ap()
    build(nc, *args, out)
    r = run_bass_kernel_spmd(nc, [arrays], core_ids=[0])
    return r.results[0]["out_y"]
```
